# Optimizing a Trainium2 kernel written in Bass

```python
import numpy as np
import jax
import jax.numpy as jnp

def _softmax(x, axis=-1):
    return jax.nn.softmax(x, axis=axis)

def _gelu(x):
    return jax.nn.gelu(x, approximate=True)

def _silu(x):
    return jax.nn.silu(x)

def _sigmoid(x):
    return jax.nn.sigmoid(x)

def _layernorm(x, axis=-1, eps=1e-05):
    m = jnp.mean(x, axis=axis, keepdims=True)
    v = jnp.var(x, axis=axis, keepdims=True)
    return (x - m) / jnp.sqrt(v + eps)

def _scatter_add(tgt, idx, src, axis=0):
    return tgt.at[idx].add(src)

def _segment_sum(src, seg, n):
    return jax.ops.segment_sum(src, seg, n)
kernel_name = 'mk_vit_tower_d1_tok_img768_r4_93bbf6'

def setup_inputs(seed: int=0):
    np.random.seed(seed)
    _w = jnp.asarray

    def _rec_inputs():
        import jax
        import jax.numpy as jnp
        _rk = jax.random.key(seed)
        x = -0.00016672 + 0.999947 * jax.random.normal(jax.random.fold_in(_rk, 1), (64, 3, 224, 224), jnp.float32)
        return x
    x = _rec_inputs()

    def _L0_tok_setup():
        import jax, jax.numpy as jnp
        import numpy as np
        PATCH = 16

        def _patchify(x, p):
            B, C, H, W = x.shape
            Hp, Wp = (H // p, W // p)
            xu = x.reshape(B, C, Hp, p, Wp, p).transpose(0, 1, 2, 4, 3, 5)
            num_patches = Hp * Wp
            return xu.reshape(B, num_patches, -1)
        key = jax.random.key(seed)
        k1, k2, k3 = jax.random.split(key, 3)
        B, C, H = (64, 3, 96)
        hidden = 192
        d = C * PATCH * PATCH
        x = jax.random.normal(k1, (B, C, H, H), dtype=jnp.float32)
        W = jax.random.normal(k2, (hidden, d), dtype=jnp.float32) * 0.02
        b = jax.random.normal(k3, (hidden,), dtype=jnp.float32) * 0.02
        return {'x': x, 'W': W, 'b': b}
    _L0_tok_all = _L0_tok_setup()
    _L0_tok_in = {k: v for k, v in _L0_tok_all.items() if k in ('W', 'b')}
    del _L0_tok_all

    def _L0_attn_setup():
        import jax, jax.numpy as jnp
        import numpy as np
        import math
        B, S, E = (2, 512, 192)
        H = 12
        V = 50257
        EPS = 1e-05

        def _layernorm(x, w):
            mu = jnp.mean(x, axis=-1, keepdims=True)
            var = jnp.mean(jnp.square(x - mu), axis=-1, keepdims=True)
            return (x - mu) * jax.lax.rsqrt(var + EPS) * w
        key = jax.random.key(seed)
        ks = jax.random.split(key, 7)
        x = jax.random.normal(ks[0], (B, S, E), dtype=jnp.float32)
        e = jax.random.normal(ks[1], (B, S, E), dtype=jnp.float32)
        p = jax.random.normal(ks[2], (B, S, E), dtype=jnp.float32)
        ln_w = jnp.ones((E,), dtype=jnp.float32)
        W_qk = 0.02 * jax.random.normal(ks[3], (H, E), dtype=jnp.float32)
        W_o = 0.02 / math.sqrt(2 * 12) * jax.random.normal(ks[4], (E, H * E), dtype=jnp.float32)
        wte = 0.02 * jax.random.normal(ks[5], (V, E), dtype=jnp.float32)
        return {'x': x, 'e': e, 'p': p, 'ln_w': ln_w, 'W_qk': W_qk, 'W_o': W_o, 'wte': wte}
    _L0_attn_all = _L0_attn_setup()
    _L0_attn_in = {k: v for k, v in _L0_attn_all.items() if k in ('e', 'p', 'ln_w', 'W_qk', 'W_o', 'wte')}
    del _L0_attn_all

    def _L0_ffn_setup():
        import jax, jax.numpy as jnp
        import numpy as np
        import math
        B, S, D = (4, 1024, 192)
        E = 8
        TOP_K = 2
        H = 512
        CAP_F = 1.25
        EPS = 1e-06
        ALPHA = 1.0
        key = jax.random.key(seed)
        k0, k1, k2, k3 = jax.random.split(key, 4)
        x = jax.random.normal(k0, (B, S, D), jnp.float32)
        gate_w = jax.random.normal(k1, (E, D), jnp.float32) * 0.02
        w13 = jax.random.normal(k2, (E, 2 * H, D), jnp.float32) * 0.02
        w2 = jax.random.normal(k3, (E, D, H), jnp.float32) * 0.02
        norm_w = jnp.ones((E, D), jnp.float32)
        return {'x': x, 'gate_w': gate_w, 'w13': w13, 'w2': w2, 'norm_w': norm_w}
    _L0_ffn_all = _L0_ffn_setup()
    _L0_ffn_in = {k: v for k, v in _L0_ffn_all.items() if k in ('gate_w', 'w13', 'w2', 'norm_w')}
    del _L0_ffn_all
    return {'x': x, 'L0_tok_W': _L0_tok_in['W'], 'L0_tok_b': _L0_tok_in['b'], 'L0_attn_e': _L0_attn_in['e'], 'L0_attn_p': _L0_attn_in['p'], 'L0_attn_ln_w': _L0_attn_in['ln_w'], 'L0_attn_W_qk': _L0_attn_in['W_qk'], 'L0_attn_W_o': _L0_attn_in['W_o'], 'L0_attn_wte': _L0_attn_in['wte'], 'L0_ffn_gate_w': _L0_ffn_in['gate_w'], 'L0_ffn_w13': _L0_ffn_in['w13'], 'L0_ffn_w2': _L0_ffn_in['w2'], 'L0_ffn_norm_w': _L0_ffn_in['norm_w']}

def reference(x, L0_tok_W, L0_tok_b, L0_attn_e, L0_attn_p, L0_attn_ln_w, L0_attn_W_qk, L0_attn_W_o, L0_attn_wte, L0_ffn_gate_w, L0_ffn_w13, L0_ffn_w2, L0_ffn_norm_w):
    import jax
    import jax.numpy as jnp

    def _L0_tok_ref(x, W, b):
        import jax, jax.numpy as jnp
        import numpy as np
        PATCH = 16

        def _patchify(x, p):
            B, C, H, W = x.shape
            Hp, Wp = (H // p, W // p)
            xu = x.reshape(B, C, Hp, p, Wp, p).transpose(0, 1, 2, 4, 3, 5)
            num_patches = Hp * Wp
            return xu.reshape(B, num_patches, -1)
        patches = _patchify(x, PATCH)
        return jnp.einsum('bnd,hd->bnh', patches, W) + b

    def _L0_attn_ref(x, e, p, ln_w, W_qk, W_o, wte):
        import jax, jax.numpy as jnp
        import numpy as np
        import math
        B, S, E = (2, 512, 192)
        H = 12
        V = 50257
        EPS = 1e-05

        def _layernorm(x, w):
            mu = jnp.mean(x, axis=-1, keepdims=True)
            var = jnp.mean(jnp.square(x - mu), axis=-1, keepdims=True)
            return (x - mu) * jax.lax.rsqrt(var + EPS) * w
        xb, sb, eb = x.shape
        xn = _layernorm(x, ln_w)
        avg_wte = jnp.mean(wte, axis=0)
        Q = xn[:, None, :, :] * W_qk[None, :, None, :]
        attn = jnp.einsum('bhse,bhte->bhst', Q, Q) / math.sqrt(eb)
        causal = jnp.tril(jnp.ones((sb, sb), dtype=bool))
        attn = jnp.where(causal[None, None], attn, -jnp.inf)
        attn = jax.nn.softmax(attn, axis=-1)
        Vv = xn[:, None, :, :] - avg_wte[None, None, None, :]
        out = jnp.einsum('bhst,bhte->bhse', attn, Vv)
        N_reg = 1.0 / jnp.arange(1, sb + 1, dtype=jnp.float32)
        out = out * N_reg[None, None, :, None]
        out = out.transpose(0, 2, 1, 3).reshape(xb, sb, H * eb)
        out = out @ W_o.T
        return out

    def _L0_ffn_ref(x, gate_w, w13, w2, norm_w):
        import jax, jax.numpy as jnp
        import numpy as np
        import math
        B, S, D = (4, 1024, 192)
        E = 8
        TOP_K = 2
        H = 512
        CAP_F = 1.25
        EPS = 1e-06
        ALPHA = 1.0
        Bx, Sx, Dx = x.shape
        N = Bx * Sx
        cap = int(math.ceil(CAP_F * TOP_K * N / E))
        xf = x.reshape(N, Dx)
        logits = xf.astype(jnp.float32) @ gate_w.T
        probs = jax.nn.softmax(logits, axis=-1)
        top_p, top_i = jax.lax.top_k(probs, TOP_K)
        w = top_p / jnp.sum(top_p, axis=-1, keepdims=True)
        flat_e = top_i.reshape(-1)
        onehot = jax.nn.one_hot(flat_e, E, dtype=jnp.int32)
        pos = jnp.take_along_axis(jnp.cumsum(onehot, axis=0) - 1, flat_e[:, None], axis=1)[:, 0]
        keep = pos < cap
        didx = flat_e * cap + jnp.minimum(pos, cap - 1)
        safe = jnp.where(keep, didx, E * cap)
        x_rep = jnp.repeat(xf, TOP_K, axis=0)
        buf = jnp.zeros((E * cap + 1, Dx), x.dtype).at[safe].set(x_rep)
        buf = buf[:-1].reshape(E, cap, Dx)
        z = 2.0 * buf
        z = z * jax.lax.rsqrt(jnp.mean(z * z, axis=-1, keepdims=True) + EPS)
        z = z * norm_w[:, None, :]
        gu = jnp.einsum('ecd,ehd->ech', z, w13)
        g, u = jnp.split(gu, 2, axis=-1)
        y = buf + ALPHA * jnp.einsum('ech,edh->ecd', jax.nn.silu(g) * u, w2)
        y_tok = y.reshape(E * cap, Dx)[didx]
        cw = (w.reshape(-1) * keep.astype(w.dtype)).astype(x.dtype)
        out = (cw[:, None] * y_tok).reshape(N, TOP_K, Dx).sum(axis=1)
        return out.reshape(Bx, Sx, Dx)
    h = _L0_tok_ref(x, L0_tok_W, L0_tok_b)
    h = h + _L0_attn_ref(_layernorm(h, axis=-1), L0_attn_e, L0_attn_p, L0_attn_ln_w, L0_attn_W_qk, L0_attn_W_o, L0_attn_wte)
    h = h + _L0_ffn_ref(_layernorm(h, axis=-1), L0_ffn_gate_w, L0_ffn_w13, L0_ffn_w2, L0_ffn_norm_w)
    return h

_drawn_inputs = setup_inputs


def setup_inputs(seed=0):
    import zlib

    import numpy as np

    out = dict(_drawn_inputs(seed))
    spreads = {'L0_attn_ln_w': (1.0, 0.6), 'L0_ffn_norm_w': (1.0, 0.6)}
    factors = {'L0_attn_W_qk': 8.0,
     'L0_attn_wte': 8.0,
     'L0_ffn_gate_w': 7.256,
     'L0_ffn_w13': 6.391,
     'L0_ffn_w2': 6.391}
    for name, (base, spread) in spreads.items():
        noise = np.random.default_rng([zlib.crc32(name.encode()), seed]).standard_normal(out[name].shape)
        drawn = base * np.exp(spread * noise) if base else spread * noise
        out[name] = jnp.asarray(drawn.astype(out[name].dtype))
    for name, factor in factors.items():
        out[name] = (out[name] * factor).astype(out[name].dtype)
    return out
```

```python
from contextlib import ExitStack

import concourse.bass as bass
from concourse import mybir

F32, F16, BF16 = mybir.dt.float32, mybir.dt.float16, mybir.dt.bfloat16
I32, U32 = mybir.dt.int32, mybir.dt.uint32
ALU, ACT, AX = mybir.AluOpType, mybir.ActivationFunctionType, mybir.AxisListType

IMAGES, CH, SIDE, PATCH = 64, 3, 224, 16
GRID = SIDE // PATCH
TOK = GRID * GRID
R = TOK // 2
E = 192
HEADS, PAIRS = 12, 6
VOCAB = 50257
N = IMAGES * TOK
EXPERTS, HID = 8, 512
CAP = -(-5 * 2 * N // (4 * EXPERTS))
SLOTS = EXPERTS * CAP
CHUNK = 5 * R
PER_EXPERT = CAP // CHUNK
CHUNKS = EXPERTS * PER_EXPERT
ROW = E + 4
META_N, META_SLOT, META_W = E, E + 1, E + 2
BIG = float(1 << 20)

QS = 64.0
PS = 2.0 ** 14
OS = 2.0 ** -5
WOS = 2.0 ** 8
ATT = 1.0 / (PS * OS * WOS)
W13S, W2S = 16.0, 16.0
SC = 1.0 / (QS * float(E) ** 0.5)
assert CAP % CHUNK == 0 and PER_EXPERT == 8

TOK_STEPS = [3, 3, 3, 3, 2, 2]
WROWS = 14
WCHUNKS = VOCAB // 128 // WROWS
WREST = VOCAB - WCHUNKS * WROWS * 128
YCOLS = 1176
YCHUNKS = N * E // 128 // YCOLS
XCOLS = SIDE - 8


class At:

    def __init__(self, half, par):
        self.half, self.par, self.t = half, par, 2 * half + par

    def shift(self, k):
        p = self.par + k
        return At(self.half + p // 2, p % 2)


def head_at(at, h):
    return at.shift(h // HEADS), h % HEADS


def build(nc, x, tok_W, tok_b, ln_w, W_qk, W_o, wte, gate_w, w13, w2, norm_w, out):
    ctx = ExitStack()
    with ctx:
        def sb(name, shape, dt=F32):
            return ctx.enter_context(nc.sbuf_tensor(name, shape, dt))

        def sem(name):
            return ctx.enter_context(nc.semaphore(name))

        H2 = nc.dram_tensor("H2", (N, E), F32).ap()
        BUF = nc.dram_tensor("BUF", (SLOTS, ROW), F32).ap()
        Y = nc.dram_tensor("Y", (2 * N, E), F32).ap()

        id32 = sb("id32", [128, 128])
        id16 = sb("id16", [128, 128], F16)
        idbf = sb("idbf", [R, R], BF16)
        maskbf = sb("maskbf", [R, R], BF16)
        before = sb("before", [R, R], F16)
        ones16 = sb("ones16", [R, R], F16)
        ones32 = sb("ones32", [128, R])
        halfneg = sb("halfneg", [R, 4])
        iota8 = sb("iota8", [R, EXPERTS])
        iotai = sb("iotai", [R, 16], I32)
        limit = sb("limit", [R, EXPERTS])
        base = sb("base", [R, EXPERTS])
        nreg = sb("nreg", [R, 2])
        tokid = sb("tokid", [R, 2])
        slotid = sb("slotid", [R, 5])
        zeros = sb("zeros", [R, 4 * E])
        empty = sb("empty", [R, 8, ROW])

        wtok = sb("wtok", [96, 8, E])
        btok = sb("btok", [R, E])
        lnw = sb("lnw", [R, E])
        avg = sb("avg", [R, E])
        q2 = sb("q2", [128, 2, HEADS])
        wo = sb("wo", [128, 2, 3 * PAIRS, E], F16)
        gateT = sb("gateT", [128, 2, EXPERTS])
        nwT = sb("nwT", [128, 2, EXPERTS])
        stream = sb("stream", [128, 3, WROWS * E])
        wpart = sb("wpart", [128, 2, E])
        raw = sb("raw", [128, 2304])
        raw2 = sb("raw2", [64, 2304])
        small = sb("small", [12, 6, 256])

        X = sb("X", [128, GRID * SIDE + 2 * 8 * TOK])
        ximg = X[0:96, 0:GRID * SIDE].rearrange("p (m w) -> p m w", w=SIDE)
        xtok = X[0:96, GRID * SIDE:].rearrange("p (c n q) -> p c n q", c=2, q=8)
        hbuf = sb("hbuf", [R, 2, 2, E])
        st1 = sb("st1", [R, 2, 6])
        mv1 = sb("mv1", [R, 2, 2])
        pw1 = sb("pw1", [R, 6, 2])
        xn = sb("xn", [R, 2, 256])
        V32 = sb("V32", [R, 2, E])
        V = sb("V", [R, 2, 2, 2, 320], F16)
        xT = sb("xT", [128, 2, 2, TOK])
        XT = sb("XT", [128, 2, 2, 2, TOK], F16)
        L = sb("L", [128, 3, 3, TOK], F16)
        P = sb("P", [R, 4, 3 * R])
        mx = sb("mx", [R, 2, 2])
        nm = sb("nm", [R, 2, 2])
        sums = sb("sums", [R, 4, 2])
        rinv = sb("rinv", [R, 4, 2])
        PT = sb("PT", [R, 2, 2, 2, 3 * R], F16)
        OT = sb("OT", [128, 2, 2, 3, TOK], F16)
        h2 = sb("h2", [R, 2, 2, E])
        st3 = sb("st3", [R, 2, 6])
        mv3 = sb("mv3", [R, 2, 2])
        pw3 = sb("pw3", [R, 7, 2])
        xf = sb("xf", [R, 2, 2, E])
        z32 = sb("z32", [R, 2, E])
        zrow = sb("zrow", [R, 2, 2, ROW])
        xfT = sb("xfT", [128, 2, TOK])
        lg = sb("lg", [R, 2, EXPERTS])
        top = sb("top", [R, 2, 8])
        topi = sb("topi", [R, 2, 8], U32)
        topf = sb("topf", [R, 2, 2])
        dif = sb("dif", [R, 2])
        edif = sb("edif", [R, 2])
        eden = sb("eden", [R, 2])
        wk = sb("wk", [R, 2, 2])
        oh = sb("oh", [R, 2, 2, EXPERTS])
        both = sb("both", [R, 2, EXPERTS], F16)
        place = sb("place", [R, 2, EXPERTS])
        over = sb("over", [R, 2, EXPERTS])
        picked = sb("picked", [R, 2, 2, EXPERTS])
        slot = sb("slot", [R, 2, 2])
        sloti = sb("sloti", [R, 2, 2, 2], I32)
        kept = sb("kept", [R, 2, 2])
        kw = sb("kw", [R, 2])
        hout = sb("hout", [R, 2, 2, E])

        rows = sb("rows", [R, 2, 5, ROW])
        zT = sb("zT", [128, 2, 3, CHUNK], F16)
        w13t = sb("w13t", [128, 2, 4, 2 * HID], F16)
        w2t = sb("w2t", [128, 2, 2, 4, E], F16)
        r13 = sb("r13", [128, 2, 256])
        r2 = sb("r2", [96, 2, 128])
        sg = raw[:, 0:2 * CHUNK].rearrange("p (k s) -> p k s", k=2)
        a32 = raw[:, 2 * CHUNK:4 * CHUNK].rearrange("p (k s) -> p k s", k=2)
        act = X[:, 0:8 * CHUNK].bitcast(F16).rearrange("p (c n k s) -> p c n k s", c=2, n=2, k=4)
        yout = stream[:].rearrange("p a b -> p (a b)")[0:R, 0:10 * E].rearrange("p (c r e) -> p c r e", c=2, r=5)
        isfirst = sb("isfirst", [R, 2, 5])
        eq = sb("eq", [R, 3, 5])
        dest = sb("dest", [R, 5])
        desti = sb("desti", [R, 2, 5, 1], I32)
        cw = sb("cw", [R, 2, 5])

        banks = ctx.enter_context(nc.psum_tensor("banks", [128, 8, 512], F32))
        pT, pOA, pOB, pPJ, pSTG, pACC = (banks[:, b, :] for b in range(2, 8))
        LG, CU = 400, 416
        zbank = banks[:, 4:6, :].rearrange("p b n -> p (b n)").bitcast(F16)
        prep = banks[:, 5, 256:512]

        c_ready = sem("c_ready")
        w_in = [sem(f"w_in{i}") for i in range(3)]
        w_red = sem("w_red")
        w_sum = sem("w_sum")
        raw_in = sem("raw_in")
        raw2_in = sem("raw2_in")
        wo_in = sem("wo_in")
        small_in = sem("small_in")
        bc_in = sem("bc_in")
        pt_done = sem("pt_done")
        pt_act = sem("pt_act")
        pt_dve = sem("pt_dve")
        empty_out = sem("empty_out")
        zeros_out = [sem(f"zeros_out{i}") for i in range(2)]
        x_in = sem("x_in")
        x_al = sem("x_al")
        tok_done = sem("tok_done")
        h_done = sem("h_done")
        pre_dve = sem("pre_dve")
        pre_pool = sem("pre_pool")
        stat1 = sem("stat1")
        r1_done = sem("r1_done")
        zs_done = sem("zs_done")
        pool_order = sem("pool_order")
        fill_ready = sem("fill_ready")
        xn_done = sem("xn_done")
        dup_done = sem("dup_done")
        v32_done = sem("v32_done")
        vh_done = sem("vh_done")
        vl_done = sem("vl_done")
        v_ready = sem("v_ready")
        xtp_done = sem("xtp_done")
        xt32_done = sem("xt32_done")
        xth_done = sem("xth_done")
        xtl_done = sem("xtl_done")
        lhi = sem("lhi")
        l_ready = sem("l_ready")
        s_done = sem("s_done")
        max_done = sem("max_done")
        nm_ready = sem("nm_ready")
        exp_done = sem("exp_done")
        r_ready = sem("r_ready")
        n_done = sem("n_done")
        t_done = sem("t_done")
        pt_hi = sem("pt_hi")
        pt_lo = sem("pt_lo")
        ot_done = sem("ot_done")
        ot_hi = sem("ot_hi")
        ot_lo = sem("ot_lo")
        pj_done = sem("pj_done")
        h2_done = sem("h2_done")
        bn3 = sem("bn3")
        stat3 = sem("stat3")
        post_pool = sem("post_pool")
        r3_done = sem("r3_done")
        xf_done = sem("xf_done")
        z32_done = sem("z32_done")
        zh_done = sem("zh_done")
        zl_done = sem("zl_done")
        ftp_done = sem("ftp_done")
        xfT_done = sem("xfT_done")
        lg_done = sem("lg_done")
        lgc_done = sem("lgc_done")
        route = sem("route")
        e_done = sem("e_done")
        both_done = sem("both_done")
        cu_done = sem("cu_done")
        slot_done = sem("slot_done")
        meta_done = sem("meta_done")
        scattered = [sem(f"scattered{i}") for i in range(2)]
        hout_done = sem("hout_done")
        hout_out = [sem(f"hout_out{i}") for i in range(2)]

        rows_in = [sem(f"rows_in{i}") for i in range(2)]
        r13_in = [sem(f"r13_in{i}") for i in range(2)]
        ft_done = sem("ft_done")
        zt_a = sem("zt_a")
        zt_b = sem("zt_b")
        gu_done = sem("gu_done")
        silu_done = sem("silu_done")
        mul_done = sem("mul_done")
        a_hi = sem("a_hi")
        a_lo = sem("a_lo")
        u13_done = sem("u13_done")
        u13_hi = sem("u13_hi")
        u13_lo = sem("u13_lo")
        u2_done = sem("u2_done")
        u2_hi = sem("u2_hi")
        u2_lo = sem("u2_lo")
        y_done = sem("y_done")
        y_ev = sem("y_ev")
        first_done = sem("first_done")
        meta_step = sem("meta_step")
        meta_ready = sem("meta_ready")
        y_out = [sem(f"y_out{i}") for i in range(2)]
        f_in = [sem(f"f_in{i}") for i in range(2)]
        f_add = sem("f_add")
        f_sum = sem("f_sum")
        f_out = [sem(f"f_out{i}") for i in range(2)]

        block = ctx.enter_context(nc.Block())

        def heads(at, h):
            a, k = head_at(at, h)
            return HEADS * a.t + k + 1

        def pairs(at, q):
            a = at.shift(q // PAIRS)
            return PAIRS * a.t + q % PAIRS + 1

        def wait(eng, s, n):
            if not (isinstance(n, int) and n <= 0):
                eng.wait_ge(s, n)

        def wait_first(eng, s, n):
            if not isinstance(n, int):
                n = eng.to_reg(n)
                eng.wait_ge(c_ready, 1)
            wait(eng, s, n)

        def over_steps(eng, step):
            step(At(-1, 1), True, False, False, False)
            step(At(0, 0), True, True, False, False)
            step(At(0, 1), True, True, True, False)
            with eng.Fori(1, IMAGES // 2 - 1) as j:
                for par in (0, 1):
                    step(At(j, par), True, True, True, True)
            last = IMAGES // 2 - 1
            step(At(last, 0), True, True, True, True)
            step(At(last, 1), False, True, True, True)
            step(At(last + 1, 0), False, False, True, True)
            step(At(last + 1, 1), False, False, False, True)

        def over_chunks(eng, chunk):
            def expert(e, pe, last):
                with eng.Fori(0, PER_EXPERT // 2 - 1) as i:
                    for pc in (0, 1):
                        chunk(e * PER_EXPERT + 2 * i + pc, pc, i, e, pe, pe, not last)
                i = PER_EXPERT // 2 - 1
                for pc in (0, 1):
                    nxt = pe if pc == 0 else (None if last else 1 - pe)
                    chunk(e * PER_EXPERT + 2 * i + pc, pc, i, e, pe, nxt, not last)

            with eng.Fori(0, EXPERTS // 2 - 1) as ep:
                expert(2 * ep, 0, False)
                expert(2 * ep + 1, 1, False)
            expert(EXPERTS - 2, 0, False)
            expert(EXPERTS - 1, 1, True)

        def fin(p, n):
            k = 3 * p + n
            return stream[:].rearrange("p a b -> p (a b)")[:, k * YCOLS:(k + 1) * YCOLS]

        @block.sync
        def _(sp):
            def load_x(at):
                wait_first(sp, x_al, 9 * at.t)
                for half in (0, 1):
                    src = x[bass.ds(at.t, 1), :, :, 8 * half:8 * half + XCOLS].rearrange("o c h w -> (o c h) w")
                    src = src.rearrange("(m g r) w -> g r m w", g=3, r=PATCH)
                    for g in range(3):
                        sp.dma_start(X[32 * g + half:32 * g + 32:2, 0:GRID * SIDE].rearrange("p (m w) -> p m w", w=SIDE)[:, :, 0:XCOLS],
                                     src[g]).then_inc(x_in, 16)

            def load_wte(k):
                if k >= 3:
                    sp.wait_ge(w_red, k - 2)
                n = WROWS * 128
                sp.dma_start(stream[:, k % 3, :], wte[k * n:(k + 1) * n, :].rearrange("(p r) e -> p (r e)", p=128)
                             ).then_inc(w_in[k % 3], 16)

            sp.dma_start(small[0:EXPERTS, 0, 0:E], gate_w).then_inc(small_in, 16)
            sp.dma_start(small[0:EXPERTS, 1, 0:E], norm_w).then_inc(small_in, 16)
            sp.dma_start(small[0:EXPERTS, 1, E:256], norm_w[:, 128:E]).then_inc(small_in, 16)
            sp.dma_start(small[0:HEADS, 2, 0:E], W_qk).then_inc(small_in, 16)
            sp.dma_start(small[0:HEADS, 2, E:256], W_qk[:, 128:E]).then_inc(small_in, 16)
            sp.dma_start(btok[:], tok_b.rearrange("(o e) -> o e", o=1).to_broadcast([R, E])).then_inc(bc_in, 16)
            sp.dma_start(lnw[:], ln_w.rearrange("(o e) -> o e", o=1).to_broadcast([R, E])).then_inc(bc_in, 16)
            sp.dma_start(raw[:, 0:768], tok_W[0:128, :]).then_inc(raw_in, 16)
            sp.dma_start(raw2[:, 0:768], tok_W[128:E, :]).then_inc(raw2_in, 16)
            load_x(At(0, 0))
            load_wte(0)
            load_wte(1)
            load_wte(2)
            sp.wait_ge(pt_done, 17)
            for r, lo, hi in ((raw, 0, 128), (raw2, 128, E)):
                src = W_o[lo:hi, :].rearrange("p (h e) -> p h e", h=HEADS)
                for col, a, b in ((0, 0, 128), (HEADS * 128, 128, E)):
                    sp.dma_start(r[:, col:col + HEADS * (b - a)].rearrange("p (h e) -> p h e", h=HEADS), src[:, :, a:b]
                                 ).then_inc(wo_in, 16)
            for k in range(3, WCHUNKS):
                load_wte(k)
            sp.wait_ge(w_red, WCHUNKS - 2)
            sp.dma_start(stream[0:WREST, WCHUNKS % 3, 0:E], wte[WCHUNKS * WROWS * 128:VOCAB, :]).then_inc(w_in[WCHUNKS % 3], 16)
            sp.wait_ge(fill_ready, 1)

            def empty_slots(first, last):
                for k in range(first, last):
                    sp.dma_start(BUF[k * 8 * R:(k + 1) * 8 * R, :].rearrange("(p r) c -> p r c", p=R), empty[:]
                                 ).then_inc(empty_out, 16)

            def step(at, nxt, main, prev, prev2):
                if nxt:
                    a = at.shift(2)
                    if not (isinstance(a.t, int) and a.t >= IMAGES):
                        load_x(a)
                if main:
                    sp.dma_start(Y[bass.ds(at.t * 4 * R, 4 * R), :].rearrange("(p r) e -> p (r e)", p=R), zeros[:]
                                 ).then_inc(zeros_out[at.par], 16)
                if isinstance(at.t, int) and at.t < 2:
                    third = -(-SLOTS // (8 * R) // 3)
                    empty_slots((at.t + 1) * third, min((at.t + 2) * third, SLOTS // (8 * R)))
                if prev2:
                    a = at.shift(-2)
                    wait_first(sp, hout_done, 2 * (a.t + 1))
                    sp.dma_start(H2[bass.ds(a.t * TOK, TOK), :].rearrange("(h p) e -> p h e", p=R),
                                 hout[:, a.par]).then_inc(hout_out[a.par], 16)

            over_steps(sp, step)

            def load_unit(v, pc, i, e):
                if not (isinstance(v, int) and v < 2):
                    wait_first(sp, u13_done, v - 1)
                    wait_first(sp, u2_done, v - 1)
                rows13 = w13[bass.ds(e, 1), bass.ds((2 * i + pc) * 128, 128), :]
                sp.dma_start(r13[:, pc, 0:E], rows13.rearrange("o p e -> (o p) e")).then_inc(r13_in[pc], 16)
                rows13 = w13[bass.ds(e, 1), bass.ds((2 * i + pc) * 128, 128), 128:E]
                sp.dma_start(r13[:, pc, E:256], rows13.rearrange("o p e -> (o p) e")).then_inc(r13_in[pc], 16)
                block2 = w2[bass.ds(e, 1), pc * 96:pc * 96 + 96, bass.ds(i * 128, 128)]
                sp.dma_start(r2[:, pc, :], block2.rearrange("o p h -> (o p) h")).then_inc(r13_in[pc], 16)

            def load_rows(c, pc):
                sp.dma_start(rows[:, pc], BUF[bass.ds(c * CHUNK, CHUNK), :].rearrange("(p r) c -> p r c", p=R)
                             ).then_inc(rows_in[pc], 16)

            for v in range(PER_EXPERT):
                load_unit(v, v % 2, v // 2, 0)
            for p in (0, 1):
                sp.wait_ge(scattered[p], 64 * (IMAGES // 2))
            load_rows(0, 0)

            def chunk(c, pc, i, e, pe, nxt, unit):
                if nxt is not None:
                    wait_first(sp, ft_done, c)
                    wait_first(sp, meta_ready, 2 * c)
                    load_rows(c + 1, 1 - pc)
                if unit:
                    load_unit(c + PER_EXPERT, pc, i, e + 1)

            over_chunks(sp, chunk)

            for p in (0, 1):
                sp.wait_ge(y_out[p], 80 * (CHUNKS // 2))
                sp.wait_ge(hout_out[p], 16 * (IMAGES // 2))
                sp.wait_ge(zeros_out[p], 16 * (IMAGES // 2))
            flat = [a.rearrange("(p r) e -> p (r e)", p=128) for a in (H2, Y[0:N, :], Y[N:2 * N, :])]
            oflat = out.rearrange("b t e -> (b t) e").rearrange("(p r) e -> p (r e)", p=128)

            def load_sum(k):
                for n in range(3):
                    sp.dma_start(fin(k % 2, n), flat[n][:, k * YCOLS:(k + 1) * YCOLS]).then_inc(f_in[k % 2], 16)

            load_sum(0)
            load_sum(1)
            for k in range(YCHUNKS):
                sp.wait_ge(f_sum, k + 1)
                sp.dma_start(oflat[:, k * YCOLS:(k + 1) * YCOLS], fin(k % 2, 0)).then_inc(f_out[k % 2], 16)
                if k + 2 < YCHUNKS:
                    sp.wait_ge(f_out[k % 2], 16 * (k // 2 + 1))
                    load_sum(k + 2)
            for p in (0, 1):
                sp.wait_ge(f_out[p], 16 * (YCHUNKS // 2))

        @block.tensor
        def _(pe):
            pe.wait_ge(c_ready, 1)
            pe.wait_ge(small_in, 80)
            pe.transpose(pT[:, 0:8], small[0:8, 0, 0:128], id32[0:8, 0:8])
            pe.transpose(pT[0:64, 8:16], small[0:8, 0, 128:192], id32[0:8, 0:8])
            pe.transpose(pT[:, 16:24], small[0:8, 1, 0:128], id32[0:8, 0:8])
            pe.transpose(pT[:, 24:32], small[0:8, 1, 128:256], id32[0:8, 0:8])
            pe.transpose(pT[:, 32:44], small[0:12, 2, 0:128], id32[0:12, 0:12])
            pe.transpose(pT[:, 44:56], small[0:12, 2, 128:256], id32[0:12, 0:12]).then_inc(pt_done, 1)
            pe.wait_ge(raw_in, 16)
            pe.wait_ge(raw2_in, 16)
            for q in range(8):
                if q >= 2:
                    pe.wait_ge(pt_act, 2 + q - 1)
                bank = banks[0:96, q % 2, 0:E]
                sel = raw[:, 0:768].rearrange("p (k q) -> p k q", q=8)[:, :, q]
                sel2 = raw2[:, 0:768].rearrange("p (k q) -> p k q", q=8)[:, :, q]
                pe.transpose(bank[:, 0:128], sel, id32[:]).then_inc(pt_done, 1)
                pe.transpose(bank[:, 128:E], sel2, id32[0:64, 0:64]).then_inc(pt_done, 1)
            pe.wait_ge(wo_in, 64)
            for q in range(PAIRS):
                for k in range(3):
                    n = 3 * q + k
                    pe.wait_ge(pt_dve, n) if n >= 2 else pe.wait_ge(pt_act, 10)
                    bank = banks[:, n % 2, 0:E]
                    for r, lo, hi in ((raw, 0, 128), (raw2, 128, E)):
                        part = 2 * q + k if k < 2 else HEADS + q
                        mm = pe.transpose(bank[:, lo:hi], r[:, part * 128:part * 128 + 128], id32[0:hi - lo, 0:hi - lo])
                    mm.then_inc(pt_done, 1)

            def gu(c_count, pc, pe_, k):
                if not (isinstance(c_count, int) and 4 * c_count + k < 2):
                    wait(pe, mul_done, 4 * c_count + k - 1)
                for u in (0, 1):
                    o = banks[:, 2 * (k % 2) + u, 0:CHUNK]
                    col = u * HID + k * 128
                    for n, (w, z) in enumerate(((0, 0), (0, 1), (1, 0), (2, 2), (3, 2))):
                        mm = pe.matmul(o, w13t[:, pe_, w, col:col + 128], zT[:, pc, z, :], start=(n == 0), stop=(n == 4))
                mm.then_inc(gu_done, 1)

            def ft(c, pc):
                wait(pe, rows_in[pc], 16 * ((c - pc) // 2 + 1) if isinstance(c, int) else c * 8 + (16 - 8 * pc))
                if not (isinstance(c, int) and c == 0):
                    wait(pe, zt_a, c)
                    wait(pe, zt_b, c)
                for m in range(5):
                    r16 = rows[:, pc, m, 0:E].bitcast(F16)
                    for n, col in enumerate((0, 256, 128)):
                        mm = pe.transpose(zbank[:, 512 * n + R * m:512 * n + R * m + R], r16[:, col:col + 128], id16[0:R, 0:R])
                mm.then_inc(ft_done, 1)

            def unit13(v, pc):
                wait(pe, r13_in[pc], 48 * ((v - pc) // 2 + 1) if isinstance(v, int) else v * 24 + (48 - 24 * pc))
                if not (isinstance(v, int) and v == 0):
                    wait(pe, u2_lo, v)
                pe.transpose(prep[:, 0:128], r13[:, pc, 0:128], id32[:])
                pe.transpose(prep[:, 128:256], r13[:, pc, 128:256], id32[:]).then_inc(u13_done, 1)

            def unit2(v, pc):
                wait(pe, u13_lo, 2 * v + 2)
                pe.transpose(prep[:, 0:96], r2[:, pc, :], id32[0:96, 0:96]).then_inc(u2_done, 1)

            for k in range(WCHUNKS):
                pe.wait_ge(w_red, k + 1)
                mm = pe.matmul(pSTG[0:R, 0:E], ones32[:], wpart[:, k % 2, :], start=(k == 0), stop=False)
                mm.then_inc(w_sum, 1)
            pe.wait_ge(w_in[WCHUNKS % 3], 16 * (WCHUNKS // 3 + 1))
            pe.matmul(pSTG[0:R, 0:E], ones32[0:WREST, :], stream[0:WREST, WCHUNKS % 3, 0:E], start=False, stop=True).then_inc(w_sum, 1)

            def tok(at, s):
                if s == 0:
                    pe.wait_ge(x_al, 9 * (at.t + 1))
                    wait(pe, h_done, at.t)
                first = sum(TOK_STEPS[:s])
                for n in range(first, first + TOK_STEPS[s]):
                    half, q = n // 8, n % 8
                    mm = pe.matmul(pACC[0:R, half * E:half * E + E], xtok[:, at.par, R * half:R * half + R, q],
                                   wtok[:, q, :], start=(q == 0), stop=(q == 7))
                if s == len(TOK_STEPS) - 1:
                    mm.then_inc(tok_done, 1)

            def scores(at, h):
                pe.wait_ge(l_ready, heads(at, h))
                if h == 0:
                    pe.wait_ge(xth_done, at.t + 1)
                wait(pe, exp_done, 2 * heads(at, h - 2))
                par = h % 2
                for half in (0, 1):
                    cols = R * (half + 1)
                    o = banks[0:R, par, R * half:R * half + cols]
                    s = slice(R * half, R * half + R)
                    Lh = L[:, h % 3]
                    terms = ((0, 0, 0), (1, 0, 0), (0, 1, 0), (2, 0, 1), (2, 1, 1))
                    for n, (lp, part, ab) in enumerate(terms):
                        pe.matmul(o, Lh[:, lp, s], XT[:, at.par, part, ab, 0:cols], start=(n == 0), stop=False)
                    mm = pe.matmul(o[:, cols - R:cols], idbf[:], maskbf[:], start=False, stop=True)
                mm.then_inc(s_done, 1)

            def turn(at, h):
                pe.wait_ge(n_done, 2 * heads(at, h))
                wait(pe, pt_lo, heads(at, h - 1))
                for k in range(3):
                    mm = pe.transpose(pT[0:R, R * k:R * k + R], P[:, h % 4, R * k:R * k + R], id32[0:R, 0:R])
                mm.then_inc(t_done, 1)

            def sum_v(at, q):
                pe.wait_ge(pt_lo, heads(at, 2 * q + 1))
                wait(pe, ot_lo, 2 * pairs(at, q - 1))
                if q == 0:
                    pe.wait_ge(v_ready, 2 * (at.t + 1))
                p = q % 2
                terms = ((0, 0), (1, 0), (0, 1))
                oA = pOA[:, 0:2 * TOK].rearrange("p (h s) -> p h s", h=2)
                for n, (vp, pp) in enumerate(terms):
                    pe.matmul(oA, V[:, at.par, vp, 0, 0:128], PT[:, p, pp, :, 0:TOK], start=(n == 0), stop=False)
                for n, (vp, pp) in enumerate(terms):
                    pe.matmul(oA[:, :, R:TOK], V[:, at.par, vp, 1, 0:128], PT[:, p, pp, :, TOK:3 * R],
                              start=False, stop=(n == 2))
                for hd in (0, 1):
                    c = 128 + 64 * hd
                    for n, (vp, pp) in enumerate(terms):
                        pe.matmul(pOB[:, 0:TOK], V[:, at.par, vp, 0, c:c + 128], PT[:, p, pp, hd, 0:TOK],
                                  start=(hd == 0 and n == 0), stop=False)
                    for n, (vp, pp) in enumerate(terms):
                        mm = pe.matmul(pOB[:, R:TOK], V[:, at.par, vp, 1, c:c + 128], PT[:, p, pp, hd, TOK:3 * R],
                                       start=False, stop=(hd == 1 and n == 2))
                mm.then_inc(ot_done, 1)

            def project(at, q):
                pe.wait_ge(ot_lo, 2 * pairs(at, q))
                if q == 0:
                    wait(pe, h2_done, at.t)
                p = q % 2
                for half in (0, 1):
                    o = pPJ[0:R, E * half:E * half + E]
                    for k in range(3):
                        for op, wp in ((0, 0), (1, 0), (0, 1)):
                            mm = pe.matmul(o, OT[:, p, op, k, R * half:R * half + R], wo[:, wp, 3 * q + k, :],
                                           start=(q == 0 and half == 0 and k == 0 and (op, wp) == (0, 0)),
                                           stop=(q == PAIRS - 1 and k == 2 and wp == 1), skip_group_check=True)
                if q == PAIRS - 1:
                    mm.then_inc(pj_done, 1)

            def step(at, nxt, main, prev, prev2):
                for s in range(HEADS):
                    if main:
                        scores(at, s)
                    a, h = head_at(at, s - 3)
                    if (main if s >= 3 else prev):
                        turn(a, h)
                    if s % 2:
                        q = (s - 5) // 2
                        if (main if q >= 0 else prev):
                            sum_v(at.shift(q // PAIRS), q % PAIRS)
                    else:
                        q = (s - 6) // 2
                        if (main if q >= 0 else prev):
                            project(at.shift(q // PAIRS), q % PAIRS)
                    if nxt and s < len(TOK_STEPS):
                        tok(at.shift(1), s)
                    if prev2 and s == 5:
                        a = at.shift(-2)
                        pe.wait_ge(both_done, a.t + 1)
                        pe.matmul(pSTG[0:R, CU:CU + 8], before[:], both[:, 0, :], start=True, stop=True)
                        pe.matmul(pSTG[0:R, CU + 8:CU + 16], before[:], both[:, 1, :], start=True, stop=False)
                        pe.matmul(pSTG[0:R, CU + 8:CU + 16], ones16[:], both[:, 0, :], start=False, stop=True)
                        pe.matmul(pSTG[0:R, CU + 16:CU + 24], ones16[:], both[:, 0, :], start=True, stop=False)
                        pe.matmul(pSTG[0:R, CU + 16:CU + 24], ones16[:], both[:, 1, :], start=False, stop=True).then_inc(cu_done, 1)
                    if nxt and s == 9:
                        a = at.shift(1)
                        pe.wait_ge(dup_done, a.t + 1)
                        wait(pe, xfT_done, 2 * (a.t - 2))
                        wait(pe, lgc_done, a.t - 2)
                        if prev2:
                            pe.wait_ge(route, 15 * at.shift(-2).t + 14)
                        for ab in (0, 1):
                            for half in (0, 1):
                                c = ab * TOK + half * R
                                mm = pe.transpose(pSTG[:, c:c + R], xn[:, half, 128 * ab:128 * ab + 128], id32[0:R, 0:R])
                        mm.then_inc(xtp_done, 1)
                    if prev and s == 10:
                        a = at.shift(-1)
                        pe.wait_ge(xf_done, 2 * (a.t + 1))
                        if nxt:
                            pe.wait_ge(xtl_done, at.t + 2)
                        elif prev2:
                            pe.wait_ge(route, 15 * at.shift(-2).t + 14)
                        for half in (0, 1):
                            pe.transpose(pSTG[:, half * R:half * R + R], xf[:, a.par, half, 0:128], id32[0:R, 0:R])
                        for half in (0, 1):
                            c = TOK + half * R
                            mm = pe.transpose(pSTG[0:64, c:c + R], xf[:, a.par, half, 128:E], id32[0:R, 0:R])
                        mm.then_inc(ftp_done, 1)
                    if prev and s == 11:
                        a = at.shift(-1)
                        pe.wait_ge(xfT_done, 2 * (a.t + 1))
                        wait(pe, lgc_done, a.t)
                        for half in (0, 1):
                            o = pSTG[0:R, LG + 8 * half:LG + 8 * half + 8]
                            hs = slice(half * R, half * R + R)
                            pe.matmul(o, xfT[:, 0, hs], gateT[:, 0, :], start=True, stop=False)
                            mm = pe.matmul(o, xfT[0:64, 1, hs], gateT[0:64, 1, :], start=False, stop=True)
                        mm.then_inc(lg_done, 1)

            over_steps(pe, step)

            for s_, n in ((exp_done, 2 * HEADS), (pt_lo, HEADS), (ot_lo, 2 * PAIRS), (h2_done, 1), (lgc_done, 1), (h_done, 1)):
                pe.wait_ge(s_, n * IMAGES)
            pe.wait_ge(route, 15 * IMAGES + 1)
            for v in range(PER_EXPERT):
                unit13(v, v % 2)
                unit2(v, v % 2)
            pe.wait_ge(u2_lo, PER_EXPERT)
            ft(0, 0)
            pe.wait_ge(zt_a, 1)
            pe.wait_ge(zt_b, 1)
            pe.wait_ge(u13_lo, 2 * PER_EXPERT)
            pe.wait_ge(u13_hi, 2 * PER_EXPERT)
            gu(0, 0, 0, 0)

            def rows_y(c, pc, pe_):
                pe.wait_ge(a_lo, 4 * c + 4)
                for u, tiles in enumerate(((0, 1), (2, 3), (4,))):
                    pe.wait_ge(y_ev, 3 * c + max(u - 1, 0))
                    for n, m in enumerate(tiles):
                        o = banks[0:R, 6 + (pc + u) % 2, E * n:E * n + E]
                        for k in range(4):
                            for ap, wp in ((0, 0), (1, 0), (0, 1)):
                                mm = pe.matmul(o, act[:, pc, ap, k, R * m:R * m + R], w2t[:, pe_, wp, k, :],
                                               start=(k == 0 and ap == 0 and wp == 0), stop=(k == 3 and wp == 1))
                    mm.then_inc(y_done, 1)

            def chunk(c, pc, i, e, pe_, nxt, unit):
                gu(c, pc, pe_, 1)
                if unit:
                    pe.wait_ge(u2_lo, c + PER_EXPERT)
                if nxt is not None:
                    ft(c + 1, 1 - pc)
                gu(c, pc, pe_, 2)
                if unit:
                    pe.wait_ge(zt_b, c + 2)
                    unit13(c + PER_EXPERT, pc)
                gu(c, pc, pe_, 3)
                if unit:
                    unit2(c + PER_EXPERT, pc)
                if nxt is not None:
                    pe.wait_ge(zt_a, c + 2)
                    pe.wait_ge(zt_b, c + 2)
                    if nxt != pe_:
                        pe.wait_ge(u13_lo, 2 * (c + PER_EXPERT + 1))
                        pe.wait_ge(u2_lo, c + PER_EXPERT + 1)
                    gu(c + 1, 1 - pc, nxt, 0)
                rows_y(c, pc, pe_)

            over_chunks(pe, chunk)

        @block.scalar
        def _(sc):
            sc.wait_ge(pt_done, 1)
            sc.wait_ge(route, 1)
            sc.activation(gateT[:, 0, :], pT[:, 0:8], ACT.Copy).then_inc(pt_act, 1)
            sc.activation(gateT[0:64, 1, :], pT[0:64, 8:16], ACT.Copy)
            sc.activation(nwT[:], pT[:, 16:32].rearrange("p (a b) -> p a b", a=2), ACT.Copy, scale=W13S).then_inc(pt_act, 1)
            for q in range(8):
                sc.wait_ge(pt_done, 3 + 2 * q)
                sc.activation(wtok[:, q, :], banks[0:96, q % 2, 0:E], ACT.Copy).then_inc(pt_act, 1)
            for n in range(3 * PAIRS):
                sc.wait_ge(pt_done, 18 + n)
                sc.activation(wo[:, 0, n, :], banks[:, n % 2, 0:E], ACT.Copy, scale=WOS).then_inc(pt_act, 1)
            def align(at, n):
                j, g = n // 3, n % 3
                lo, hi = -(-(GRID * g - j) // 3), (GRID * g + GRID - 1 - j) // 3 + 1
                if n == 0:
                    sc.wait_ge(x_in, 96 * (at.t + 1))
                    wait(sc, tok_done, at.t - 1)
                col = PATCH * (3 * lo + j - GRID * g)
                src = ximg[32 * g:32 * g + 32, :, col:col + 3 * PATCH * (hi - lo - 1) + 8]
                src = bass.AP(src.tensor, src.offset, [*src.ap[:2], [3 * PATCH, hi - lo], [1, 8]])
                dst = xtok[32 * j:32 * j + 32, at.par].rearrange("p (m i) q -> p m i q", i=GRID)[:, :, lo:hi, :]
                sc.activation(dst, src, ACT.Copy).then_inc(x_al, 1)

            for n in range(9):
                align(At(0, 0), n)
            sc.wait_ge(w_sum, WCHUNKS + 1)
            sc.activation(avg[:], pSTG[0:R, 0:E], ACT.Copy, scale=1.0 / VOCAB).then_inc(pt_act, 1)

            def step(at, nxt, main, prev, prev2):
                for s in range(HEADS):
                    a, h = head_at(at, s - 1)
                    if (main if s >= 1 else prev):
                        sc.wait_ge(nm_ready, heads(a, h))
                        for half in (0, 1):
                            cols = slice(R * half, R * half + R * (half + 1))
                            sc.activation(P[:, h % 4, cols], banks[0:R, h % 2, cols], ACT.Exp, bias=nm[:, h % 2, half:half + 1],
                                          scale=SC, accum_out=sums[:, h % 4, half:half + 1]).then_inc(exp_done, 1)
                    a, h = head_at(at, s - 3)
                    if (main if s >= 3 else prev):
                        sc.wait_ge(t_done, heads(a, h))
                        sc.activation(PT[:, (h // 2) % 2, 0, h % 2, :], pT[0:R, 0:3 * R], ACT.Copy).then_inc(pt_hi, 1)
                    q = (s - 5) // 2
                    if s % 2 and (main if q >= 0 else prev):
                        a, k = at.shift(q // PAIRS), q % PAIRS
                        sc.wait_ge(ot_done, pairs(a, k))
                        sc.activation(OT[:, k % 2, 0, 0:2, :], pOA[:, 0:2 * TOK].rearrange("p (h s) -> p h s", h=2),
                                      ACT.Copy, scale=OS).then_inc(ot_hi, 1)
                        sc.activation(OT[:, k % 2, 0, 2, :], pOB[:, 0:TOK], ACT.Copy, scale=OS).then_inc(ot_hi, 1)
                    if nxt and 2 <= s < 11:
                        a = at.shift(2)
                        if not (isinstance(a.t, int) and a.t >= IMAGES):
                            align(a, s - 2)
                    if prev2 and s == 2:
                        a = at.shift(-2)
                        sc.wait_ge(route, 15 * a.t + 6)
                        sc.activation(edif[:], dif[:], ACT.Exp).then_inc(e_done, 1)
                    if nxt and s == 9:
                        a = at.shift(1)
                        sc.wait_ge(xtp_done, a.t + 1)
                        stg = pSTG[:, 0:2 * TOK].rearrange("p (a s) -> p a s", a=2)
                        sc.activation(xT[:, a.par], stg, ACT.Copy).then_inc(xt32_done, 1)
                        sc.activation(XT[:, a.par, 0], stg, ACT.Copy).then_inc(xth_done, 1)
                    if prev and s == 9:
                        a = at.shift(-1)
                        sc.wait_ge(z32_done, 2 * (a.t + 1))
                        if not (isinstance(a.half, int) and a.half == 0):
                            sc.wait_ge(scattered[a.par], 64 * a.half)
                        sc.activation(zrow[:, a.par, :, 0:E // 2].bitcast(F16), z32[:], ACT.Copy).then_inc(zh_done, 1)
                    if prev and s == 10:
                        a = at.shift(-1)
                        sc.wait_ge(ftp_done, a.t + 1)
                        sc.activation(xfT[:, 0, :], pSTG[:, 0:TOK], ACT.Copy).then_inc(xfT_done, 1)
                        sc.activation(xfT[0:64, 1, :], pSTG[0:64, TOK:2 * TOK], ACT.Copy).then_inc(xfT_done, 1)

            over_steps(sc, step)

            def unit13(v, pe_, blk, e):
                wait_first(sc, u13_done, v + 1)
                for ab in (0, 1):
                    sc.activation(w13t[:, pe_, 2 * ab, bass.ds(blk * 128, 128)], prep[:, 128 * ab:128 * ab + 128],
                                  ACT.Copy, scale=nwT[:, ab, bass.ds(e, 1)]).then_inc(u13_hi, 1)

            def unit2(v, pc, pe_, i):
                sc.wait_ge(u2_done, v + 1)
                sc.activation(w2t[:, pe_, 0, bass.ds(i, 1), 96 * pc:96 * pc + 96].rearrange("p o d -> p (o d)"), prep[:, 0:96],
                              ACT.Copy, scale=W2S).then_inc(u2_hi, 1)

            def silu(q, k):
                sc.wait_ge(gu_done, q + 1)
                if not (isinstance(q, int) and q < 2):
                    wait(sc, mul_done, q - 1)
                sc.activation(sg[:, k % 2, :], banks[:, 2 * (k % 2), 0:CHUNK], ACT.Silu, scale=1.0 / W13S).then_inc(silu_done, 1)

            def z_parts(c, pc):
                sc.wait_ge(ft_done, c + 1)
                sc.activation(zT[:, pc, 0:2, :], zbank[:, 0:1024].rearrange("p (a s) -> p a s", a=2)[:, :, 0:CHUNK],
                              ACT.Copy).then_inc(zt_a, 1)

            for v in range(PER_EXPERT):
                unit13(v, 0, v, 0)
                unit2(v, v % 2, 0, v // 2)
            z_parts(0, 0)
            silu(0, 0)

            def chunk(c, pc, i, e, pe_, nxt, unit):
                silu(4 * c + 1, 1)
                if nxt is not None:
                    z_parts(c + 1, 1 - pc)
                silu(4 * c + 2, 0)
                if unit:
                    unit13(c + PER_EXPERT, 1 - pe_, 2 * i + pc, e + 1)
                silu(4 * c + 3, 1)
                if unit:
                    unit2(c + PER_EXPERT, pc, 1 - pe_, i)
                if nxt is not None:
                    silu(4 * c + 4, 0)
                if not (isinstance(c, int) and c < 2):
                    wait(sc, y_out[pc], 40 * c - 40 * pc)
                sc.wait_ge(meta_ready, 2 * (c + 1))
                for u, tiles in enumerate(((0, 1), (2, 3), (4,))):
                    sc.wait_ge(y_done, 3 * c + u + 1)
                    for n, m in enumerate(tiles):
                        ev = sc.activation(yout[:, pc, m, :], banks[0:R, 6 + (pc + u) % 2, E * n:E * n + E], ACT.Copy,
                                           scale=cw[:, pc, m:m + 1])
                    ev.then_inc(y_ev, 1)

            over_chunks(sc, chunk)

        @block.vector
        def _(ve):
            ve.wait_ge(pt_done, 1)
            ve.tensor_copy(q2[:], pT[:, 32:56].rearrange("p (a b) -> p a b", a=2)).then_inc(route, 1)
            ve.wait_ge(route, 1)
            ve.scalar_tensor_tensor(out=q2[:], in0=q2[:], scalar=QS, in1=q2[:], op0=ALU.mult, op1=ALU.mult).then_inc(pt_dve, 1)
            wte_next = [0]

            def wte_rows():
                k = wte_next[0]
                if k < WCHUNKS:
                    ve.wait_ge(w_in[k % 3], 16 * (k // 3 + 1))
                    if k >= 2:
                        ve.wait_ge(w_sum, k - 1)
                    ve.tensor_reduce(wpart[:, k % 2, :], stream[:, k % 3, :].rearrange("p (r e) -> p e r", e=E), AX.X, ALU.add).then_inc(w_red, 1)
                    wte_next[0] += 1

            wte_rows()
            wte_rows()
            for n in range(3 * PAIRS):
                ve.wait_ge(pt_act, 11 + n)
                ve.scalar_tensor_tensor(out=wo[:, 1, n, :], in0=banks[:, n % 2, 0:E], scalar=WOS, in1=wo[:, 0, n, :],
                                        op0=ALU.mult, op1=ALU.subtract).then_inc(pt_dve, 1)
            while wte_next[0] < WCHUNKS:
                wte_rows()

            def softmax_max(at, h):
                ve.wait_ge(s_done, heads(at, h))
                for half in (0, 1):
                    ve.tensor_reduce(mx[:, h % 2, half:half + 1], banks[0:R, h % 2, R * half:R * half + R * (half + 1)],
                                     AX.X, ALU.max).then_inc(max_done, 1)

            def low_l(at, h):
                n = 2 * heads(at, h)
                ve.wait_ge(lhi, n)
                if h == 0:
                    ve.wait_ge(xt32_done, at.t + 1)
                Lh = L[:, h % 3]
                ve.scalar_tensor_tensor(out=Lh[:, 1, :], in0=xT[:, at.par, 0, :], scalar=q2[:, 0, h:h + 1], in1=Lh[:, 0, :],
                                        op0=ALU.mult, op1=ALU.subtract)
                ve.scalar_tensor_tensor(out=Lh[64:128, 2, :], in0=xT[64:128, at.par, 1, :], scalar=q2[64:128, 1, h:h + 1],
                                        in1=Lh[64:128, 2, :], op0=ALU.mult, op1=ALU.subtract).then_inc(l_ready, 1)

            def step(at, nxt, main, prev, prev2):
                up, down, past = at.shift(1), at.shift(-1), at.shift(-2)
                rt = 15 * past.t + 1
                for s in range(HEADS):
                    a, h = head_at(at, s - 1)
                    soft = (main if s >= 1 else prev)
                    if soft:
                        softmax_max(a, h)
                    if (main if s < HEADS - 1 else nxt):
                        low_l(*head_at(at, s + 1))
                    if soft:
                        ve.wait_ge(max_done, 2 * heads(a, h))
                        ve.tensor_scalar(nm[:, h % 2, :], mx[:, h % 2, :], -SC, None, ALU.mult).then_inc(nm_ready, 1)
                    a, h = head_at(at, s - 2)
                    if (main if s >= 2 else prev):
                        ve.wait_ge(exp_done, 2 * heads(a, h))
                        ve.reciprocal(rinv[:, h % 4, :], sums[:, h % 4, :]).then_inc(r_ready, 1)
                    a, h = head_at(at, s - 3)
                    if (main if s >= 3 else prev):
                        ve.wait_ge(pt_hi, heads(a, h))
                        ve.tensor_tensor(PT[:, (h // 2) % 2, 1, h % 2, :], pT[0:R, 0:3 * R], PT[:, (h // 2) % 2, 0, h % 2, :],
                                         ALU.subtract).then_inc(pt_lo, 1)
                    if prev and s == 5:
                        ve.wait_ge(pj_done, down.t + 1)
                        ve.scalar_tensor_tensor(out=h2[:, down.par].rearrange("p a e -> p (a e)"), in0=pPJ[0:R, 0:2 * E],
                                                scalar=ATT, in1=hbuf[:, down.par].rearrange("p a e -> p (a e)"),
                                                op0=ALU.mult, op1=ALU.add).then_inc(h2_done, 1)
                    q = (s - 5) // 2
                    if s % 2 and (main if q >= 0 else prev):
                        a, k = at.shift(q // PAIRS), q % PAIRS
                        ve.wait_ge(ot_hi, 2 * pairs(a, k))
                        ve.scalar_tensor_tensor(out=OT[:, k % 2, 1, 0:2, :].rearrange("p h s -> p (h s)"), in0=pOA[:, 0:2 * TOK], scalar=OS,
                                                in1=OT[:, k % 2, 0, 0:2, :].rearrange("p h s -> p (h s)"),
                                                op0=ALU.mult, op1=ALU.subtract).then_inc(ot_lo, 1)
                        ve.scalar_tensor_tensor(out=OT[:, k % 2, 1, 2, :], in0=pOB[:, 0:TOK], scalar=OS, in1=OT[:, k % 2, 0, 2, :],
                                                op0=ALU.mult, op1=ALU.subtract).then_inc(ot_lo, 1)
                    if prev and s == 5:
                        ve.wait_ge(h2_done, down.t + 1)
                        for half in (0, 1):
                            ve.bn_stats(st3[:, half, :], h2[:, down.par, half, :]).then_inc(bn3, 1)
                    if prev and s == 6:
                        wait_first(ve, bn3, 2 * (down.t + 1))
                        for half in (0, 1):
                            ve.bn_aggr(mv3[:, half, :], st3[:, half, :]).then_inc(stat3, 1)
                    if prev and s == 7:
                        ve.wait_ge(r3_done, down.t + 1)
                        for half in (0, 1):
                            ve.tensor_scalar(xf[:, down.par, half, :], h2[:, down.par, half, :], mv3[:, half, 0:1],
                                             pw3[:, 1, half:half + 1], ALU.subtract, ALU.mult).then_inc(xf_done, 1)
                    if prev and s == 8:
                        ve.wait_ge(xf_done, 2 * (down.t + 1))
                        ve.wait_ge(zs_done, down.t + 1)
                        wait(ve, zl_done, 2 * down.t)
                        for half in (0, 1):
                            ve.tensor_scalar(z32[:, half, :], xf[:, down.par, half, :], pw3[:, 6, half:half + 1],
                                             None, ALU.mult).then_inc(z32_done, 1)
                    if prev and s == 10:
                        ve.wait_ge(zh_done, down.t + 1)
                        zr = zrow[:, down.par, :, 0:E].bitcast(F16)
                        ve.tensor_tensor(zr[:, :, 256:384], z32[:, :, 0:128], zr[:, :, 0:128], ALU.subtract).then_inc(zl_done, 1)
                        ve.tensor_tensor(zr[:, :, E:256], z32[:, :, 128:E], zr[:, :, 128:E], ALU.subtract).then_inc(zl_done, 1)
                    if prev and s == 11:
                        ve.wait_ge(lg_done, down.t + 1)
                        ve.tensor_copy(lg[:], pSTG[0:R, LG:LG + 16].rearrange("p (a b) -> p a b", a=2)).then_inc(lgc_done, 1)
                    if nxt and s == 6:
                        ve.wait_ge(tok_done, up.t + 1)
                        if isinstance(up.t, int) and up.t == 0:
                            ve.wait_ge(bc_in, 32)
                        ve.tensor_tensor(hbuf[:, up.par], pACC[0:R, 0:2 * E].rearrange("p (a e) -> p a e", a=2),
                                         btok[:].rearrange("p (o e) -> p o e", o=1).to_broadcast([R, 2, E]), ALU.add).then_inc(h_done, 1)
                    if nxt and s == 7:
                        ve.wait_ge(h_done, up.t + 1)
                        for half in (0, 1):
                            ve.bn_stats(st1[:, half, :], hbuf[:, up.par, half, :]).then_inc(pre_dve, 1)
                        wait_first(ve, pre_dve, 2 * (up.t + 1))
                        for half in (0, 1):
                            ve.bn_aggr(mv1[:, half, :], st1[:, half, :]).then_inc(stat1, 1)
                    if nxt and s == 8:
                        ve.wait_ge(r1_done, up.t + 1)
                        wait(ve, xn_done, 3 * up.t)
                        wait(ve, v32_done, up.t)
                        wait(ve, xtp_done, up.t)
                        for half in (0, 1):
                            ve.tensor_scalar(xn[:, half, 0:E], hbuf[:, up.par, half, :], mv1[:, half, 0:1],
                                             pw1[:, 5, half:half + 1], ALU.subtract, ALU.mult).then_inc(xn_done, 1)
                        ve.wait_ge(xn_done, 3 * up.t + 2)
                        ve.tensor_tensor(xn[:, :, 0:E], xn[:, :, 0:E], lnw[:].rearrange("p (o e) -> p o e", o=1).to_broadcast([R, 2, E]),
                                         ALU.mult).then_inc(xn_done, 1)
                    if nxt and s == 9:
                        ve.wait_ge(xth_done, up.t + 1)
                        ve.tensor_tensor(XT[:, up.par, 1], pSTG[:, 0:2 * TOK].rearrange("p (a s) -> p a s", a=2), XT[:, up.par, 0],
                                         ALU.subtract).then_inc(xtl_done, 1)
                    if nxt and s == 10:
                        ve.wait_ge(vh_done, up.t + 1)
                        ve.tensor_tensor(V[:, up.par, 1, :, 0:E], V32[:], V[:, up.par, 0, :, 0:E], ALU.subtract).then_inc(vl_done, 1)
                    if prev2:
                        if s == 0:
                            wait_first(ve, lgc_done, past.t + 1)
                            for half in (0, 1):
                                ve.max(top[:, half, :], lg[:, half, :]).then_inc(route, 1)
                        if s == 1:
                            wait_first(ve, route, rt + 2)
                            for half in (0, 1):
                                ve.max_index(topi[:, half, :], top[:, half, :], lg[:, half, :]).then_inc(route, 1)
                            ve.tensor_tensor(dif[:], top[:, :, 1], top[:, :, 0], ALU.subtract).then_inc(route, 1)
                        if s == 2:
                            ve.wait_ge(route, rt + 5)
                            ve.tensor_copy(topf[:], topi[:, :, 0:2]).then_inc(route, 1)
                        if s == 3:
                            ve.wait_ge(route, rt + 6)
                            for half in (0, 1):
                                ve.tensor_tensor(oh[:, half], iota8[:].rearrange("p (o e) -> p o e", o=1).to_broadcast([R, 2, EXPERTS]),
                                                 topf[:, half].rearrange("p (k o) -> p k o", o=1).to_broadcast([R, 2, EXPERTS]),
                                                 ALU.is_equal).then_inc(route, 1)
                            ve.wait_ge(e_done, past.t + 1)
                            ve.tensor_scalar(eden[:], edif[:], 1.0, None, ALU.add).then_inc(route, 1)
                        if s == 4:
                            ve.wait_ge(route, rt + 9)
                            wait(ve, meta_done, 2 * past.t)
                            ve.tensor_tensor(both[:], oh[:, :, 0, :], oh[:, :, 1, :], ALU.add).then_inc(both_done, 1)
                            ve.reciprocal(wk[:, :, 0], eden[:]).then_inc(route, 1)
                        if s == 5:
                            ve.wait_ge(route, rt + 10)
                            ve.tensor_tensor(wk[:, :, 1], edif[:], wk[:, :, 0], ALU.mult).then_inc(route, 1)
                        if s == 6:
                            ve.wait_ge(cu_done, past.t + 1)
                            ve.tensor_tensor(place[:], pSTG[0:R, CU:CU + 16].rearrange("p (a b) -> p a b", a=2),
                                             base[:].rearrange("p (o e) -> p o e", o=1).to_broadcast([R, 2, EXPERTS]), ALU.add).then_inc(route, 1)
                            ve.wait_ge(route, rt + 12)
                            ve.tensor_tensor(base[:], pSTG[0:R, CU + 16:CU + 24], base[:], ALU.add).then_inc(route, 1)
                            ve.tensor_tensor(over[:], place[:], limit[:].rearrange("p (o e) -> p o e", o=1).to_broadcast([R, 2, EXPERTS]),
                                             ALU.is_ge).then_inc(route, 1)
                        if s == 7:
                            ve.wait_ge(route, rt + 14)
                            ve.scalar_tensor_tensor(out=place[:], in0=over[:], scalar=BIG, in1=place[:], op0=ALU.mult, op1=ALU.add
                                                    ).then_inc(route, 1)
                            ve.wait_ge(route, rt + 15)
                            wait(ve, slot_done, 7 * past.t)
                            for k in (0, 1):
                                ve.tensor_tensor(picked[:, :, k, :], oh[:, :, k, :], place[:], ALU.mult).then_inc(slot_done, 1)
                        if s == 8:
                            ve.wait_ge(slot_done, 7 * past.t + 2)
                            ve.tensor_reduce(slot[:], picked[:], AX.X, ALU.add).then_inc(slot_done, 1)
                            ve.wait_ge(slot_done, 7 * past.t + 3)
                            if not (isinstance(past.half, int) and past.half == 0):
                                ve.wait_ge(scattered[past.par], 64 * past.half)
                            ve.tensor_copy(sloti[:, past.par], slot[:]).then_inc(slot_done, 1)
                            for half in (0, 1):
                                ve.scalar_tensor_tensor(out=kept[:, half, :], in0=slot[:, half, :], scalar=BIG, in1=wk[:, half, :],
                                                        op0=ALU.is_lt, op1=ALU.mult).then_inc(slot_done, 1)
                        if s == 9:
                            ve.wait_ge(slot_done, 7 * past.t + 6)
                            ve.tensor_tensor(kw[:], kept[:, :, 0], kept[:, :, 1], ALU.add).then_inc(slot_done, 1)
                        if s == 10:
                            ve.wait_ge(slot_done, 7 * past.t + 7)
                            if not (isinstance(past.half, int) and past.half == 0):
                                ve.wait_ge(hout_out[past.par], 16 * past.half)
                            for half in (0, 1):
                                ve.scalar_tensor_tensor(out=hout[:, past.par, half, :], in0=xf[:, past.par, half, :], scalar=kw[:, half:half + 1],
                                                        in1=h2[:, past.par, half, :], op0=ALU.mult, op1=ALU.add).then_inc(hout_done, 1)

            over_steps(ve, step)

            def unit13(v, pe_, blk, e):
                ve.wait_ge(u13_hi, 2 * v + 2)
                for ab in (0, 1):
                    ve.scalar_tensor_tensor(out=w13t[:, pe_, 2 * ab + 1, bass.ds(blk * 128, 128)], in0=prep[:, 128 * ab:128 * ab + 128],
                                            scalar=nwT[:, ab, bass.ds(e, 1)], in1=w13t[:, pe_, 2 * ab, bass.ds(blk * 128, 128)],
                                            op0=ALU.mult, op1=ALU.subtract).then_inc(u13_lo, 1)

            def unit2(v, pc, pe_, i):
                ve.wait_ge(u2_hi, v + 1)
                hi, lo = (w2t[:, pe_, n, bass.ds(i, 1), 96 * pc:96 * pc + 96].rearrange("p o d -> p (o d)") for n in (0, 1))
                ve.scalar_tensor_tensor(out=lo, in0=prep[:, 0:96], scalar=W2S, in1=hi,
                                        op0=ALU.mult, op1=ALU.subtract).then_inc(u2_lo, 1)

            def z_rest(c, pc):
                ve.wait_ge(ft_done, c + 1)
                ve.tensor_copy(zT[:, pc, 2, :], zbank[:, 1024:1024 + CHUNK]).then_inc(zt_b, 1)
                wait(ve, first_done, 2 * c)
                ve.tensor_tensor(isfirst[:, pc, :], rows[:, pc, :, META_SLOT], slotid[:], ALU.is_equal).then_inc(first_done, 1)
                ve.wait_ge(first_done, 2 * c + 1)
                ve.tensor_scalar(slotid[:], slotid[:], float(CHUNK), None, ALU.add).then_inc(first_done, 1)

            def gate(q, k):
                ve.wait_ge(silu_done, q + 1)
                if not (isinstance(q, int) and q < 2):
                    wait(ve, a_lo, q - 1)
                ve.tensor_tensor(a32[:, k % 2, :], banks[:, 2 * (k % 2) + 1, 0:CHUNK], sg[:, k % 2, :], ALU.mult).then_inc(mul_done, 1)

            def low_a(q, pc, k):
                ve.wait_ge(a_hi, q + 1)
                ve.tensor_tensor(act[:, pc, 1, k, :], a32[:, k % 2, :], act[:, pc, 0, k, :], ALU.subtract).then_inc(a_lo, 1)

            for v in range(PER_EXPERT):
                unit13(v, 0, v, 0)
                unit2(v, v % 2, 0, v // 2)
            z_rest(0, 0)
            gate(0, 0)

            def chunk(c, pc, i, e, pe_, nxt, unit):
                gate(4 * c + 1, 1)
                low_a(4 * c, pc, 0)
                if nxt is not None:
                    z_rest(c + 1, 1 - pc)
                gate(4 * c + 2, 0)
                low_a(4 * c + 1, pc, 1)
                if unit:
                    unit13(c + PER_EXPERT, 1 - pe_, 2 * i + pc, e + 1)
                gate(4 * c + 3, 1)
                low_a(4 * c + 2, pc, 2)
                if unit:
                    unit2(c + PER_EXPERT, pc, 1 - pe_, i)
                if nxt is not None:
                    gate(4 * c + 4, 0)
                low_a(4 * c + 3, pc, 3)

            over_chunks(ve, chunk)

            for k in range(YCHUNKS):
                ve.wait_ge(f_in[k % 2], 48 * (k // 2 + 1))
                ve.tensor_tensor(fin(k % 2, 1), fin(k % 2, 1), fin(k % 2, 2), ALU.add).then_inc(f_add, 1)
                ve.wait_ge(f_add, k + 1)
                ve.tensor_tensor(fin(k % 2, 0), fin(k % 2, 0), fin(k % 2, 1), ALU.add).then_inc(f_sum, 1)

        @block.gpsimd
        def _(po):
            class Order:

                def __init__(self, s, start=0):
                    self.s, self.n = s, start

                def __call__(self, ins):
                    self.n = self.n + 1
                    ins.then_inc(self.s, 1)
                    wait_first(po, self.s, self.n)

            own = Order(pool_order)

            def select(t, op, fill, b, cm, step_, width):
                return po.affine_select(out=t, in_=t, compare_op=op, fill=fill, base=b, pattern=[[step_, width]], channel_multiplier=cm)

            own(po.memset(zeros[:], 0.0))
            own(po.memset(empty[:], 0.0))
            own(po.memset(empty[:, :, META_N:META_N + 1], BIG))
            po.memset(halfneg[:], -0.5).then_inc(fill_ready, 1)
            own(po.memset(ones32[:], 1.0))
            own(po.memset(ones16[:], 1.0))
            own(po.memset(id32[:], 0.0))
            own(select(id32[:], ALU.not_equal, 1.0, 0, 1, -1, 128))
            own(po.memset(id16[:], 0.0))
            own(select(id16[:], ALU.not_equal, 1.0, 0, 1, -1, 128))
            own(po.memset(idbf[:], 0.0))
            own(select(idbf[:], ALU.not_equal, 1.0, 0, 1, -1, R))
            own(po.memset(maskbf[:], 0.0))
            own(select(maskbf[:], ALU.is_ge, -1e30, 0, 1, -1, R))
            own(po.memset(before[:], 0.0))
            own(select(before[:], ALU.is_ge, 1.0, 0, 1, -1, R))
            own(po.memset(V[:], 0.0))
            own(po.iota(iotai[:, 0:8], pattern=[[1, 8]], base=0, channel_multiplier=0))
            own(po.tensor_copy(iota8[:], iotai[:, 0:8]))
            own(po.iota(iotai[:, 0:8], pattern=[[CAP, 8]], base=0, channel_multiplier=0))
            own(po.tensor_copy(base[:], iotai[:, 0:8]))
            own(po.tensor_scalar(limit[:], base[:], float(CAP), None, ALU.add))
            own(po.iota(iotai[:, 8:10], pattern=[[R, 2]], base=0, channel_multiplier=1))
            own(po.tensor_copy(tokid[:], iotai[:, 8:10]))
            own(po.iota(iotai[:, 10:15], pattern=[[1, 5]], base=0, channel_multiplier=5))
            own(po.tensor_copy(slotid[:], iotai[:, 10:15]))
            own(po.tensor_scalar(nreg[:], tokid[:], 1.0, None, ALU.add))
            own(po.memset(pw1[:, 0, :], -1.0))
            own(po.tensor_tensor(nreg[:], nreg[:], pw1[:, 0, :], ALU.pow))
            po.tensor_scalar(nreg[:], nreg[:], PS, None, ALU.mult).then_inc(c_ready, 1)
            po.wait_ge(c_ready, 1)
            po.wait_ge(pt_dve, 1)
            po.wait_ge(pt_act, 2 + 8 + 3 * PAIRS + 1)

            def high_l(at, h):
                if h == 0:
                    wait_first(po, xt32_done, at.t + 1)
                wait_first(po, s_done, heads(at, h - 3))
                po.tensor_scalar(L[:, h % 3, 0, :], xT[:, at.par, 0, :], q2[:, 0, h:h + 1], None, ALU.mult).then_inc(lhi, 1)
                po.tensor_scalar(L[:, h % 3, 2, :], xT[:, at.par, 1, :], q2[:, 1, h:h + 1], None, ALU.mult).then_inc(lhi, 1)

            def step(at, nxt, main, prev, prev2):
                up, down, past = at.shift(1), at.shift(-1), at.shift(-2)
                for s in range(HEADS):
                    if (main if s < HEADS - 1 else nxt):
                        high_l(*head_at(at, s + 1))
                    a, h = head_at(at, s - 2)
                    if (main if s >= 2 else prev):
                        wait_first(po, r_ready, heads(a, h))
                        for half in (0, 1):
                            cols = slice(R * half, R * half + R * (half + 1))
                            po.tensor_scalar(P[:, h % 4, cols], P[:, h % 4, cols], rinv[:, h % 4, half:half + 1],
                                             nreg[:, half:half + 1], ALU.mult, ALU.mult).then_inc(n_done, 1)
                    if prev and s == 6:
                        wait_first(po, stat3, 2 * (down.t + 1))
                        v = mv3[:, :, 1]
                        own = Order(post_pool, 5 * down.t)
                        own(po.tensor_scalar(pw3[:, 0, :], v, 1e-5, None, ALU.add))
                        po.tensor_tensor(pw3[:, 1, :], pw3[:, 0, :], halfneg[:, 0:2], ALU.pow).then_inc(r3_done, 1)
                        wait_first(po, r3_done, down.t + 1)
                        own(po.tensor_tensor(pw3[:, 2, :], pw3[:, 1, :], pw3[:, 1, :], ALU.mult))
                        own(po.tensor_tensor(pw3[:, 3, :], pw3[:, 2, :], v, ALU.mult))
                        own(po.tensor_scalar(pw3[:, 4, :], pw3[:, 3, :], 4.0, 1e-6, ALU.mult, ALU.add))
                        own(po.tensor_tensor(pw3[:, 5, :], pw3[:, 4, :], halfneg[:, 0:2], ALU.pow))
                        po.tensor_scalar(pw3[:, 6, :], pw3[:, 5, :], 2.0, None, ALU.mult).then_inc(zs_done, 1)
                    if nxt and s == 7:
                        wait_first(po, stat1, 2 * (up.t + 1))
                        v = mv1[:, :, 1]
                        own = Order(pre_pool, 6 * up.t)
                        own(po.tensor_scalar(pw1[:, 0, :], v, 1e-5, None, ALU.add))
                        own(po.tensor_tensor(pw1[:, 1, :], pw1[:, 0, :], halfneg[:, 0:2], ALU.pow))
                        own(po.tensor_tensor(pw1[:, 2, :], pw1[:, 1, :], pw1[:, 1, :], ALU.mult))
                        own(po.tensor_tensor(pw1[:, 3, :], pw1[:, 2, :], v, ALU.mult))
                        own(po.tensor_scalar(pw1[:, 2, :], pw1[:, 3, :], 1e-5, None, ALU.add))
                        own(po.tensor_tensor(pw1[:, 4, :], pw1[:, 2, :], halfneg[:, 0:2], ALU.pow))
                        po.tensor_tensor(pw1[:, 5, :], pw1[:, 4, :], pw1[:, 1, :], ALU.mult).then_inc(r1_done, 1)
                    if nxt and s == 8:
                        wait_first(po, xn_done, 3 * (up.t + 1))
                        po.tensor_copy(xn[:, :, E:256], xn[:, :, 128:E]).then_inc(dup_done, 1)
                        wait_first(po, vl_done, up.t)
                        po.tensor_tensor(V32[:], xn[:, :, 0:E], avg[:].rearrange("p (o e) -> p o e", o=1).to_broadcast([R, 2, E]),
                                         ALU.subtract).then_inc(v32_done, 1)
                    if nxt and s == 9:
                        wait_first(po, v32_done, up.t + 1)
                        wait_first(po, ot_done, PAIRS * (up.t - 1))
                        po.tensor_copy(V[:, up.par, 0, :, 0:E], V32[:]).then_inc(vh_done, 1)
                        po.tensor_copy(V[:, up.par, 0, :, 256:320], V32[:, :, 128:E]).then_inc(v_ready, 1)
                    if nxt and s == 11:
                        wait_first(po, vl_done, up.t + 1)
                        po.tensor_copy(V[:, up.par, 1, :, 256:320], V[:, up.par, 1, :, 128:E]).then_inc(v_ready, 1)
                    if isinstance(at.t, int) and at.t == 1 and s == 11:
                        wait_first(po, empty_out, 16 * (SLOTS // (8 * R)))
                    if prev2 and s == 9:
                        wait_first(po, slot_done, 7 * past.t + 4)
                        po.tensor_copy(zrow[:, past.par, :, META_N], tokid[:])
                        po.tensor_copy(zrow[:, past.par, :, META_SLOT], slot[:, :, 0])
                        po.tensor_copy(zrow[:, past.par, :, META_W:META_W + 2], wk[:]).then_inc(meta_done, 1)
                        wait_first(po, meta_done, 2 * past.t + 1)
                        po.tensor_scalar(tokid[:], tokid[:], float(TOK), None, ALU.add).then_inc(meta_done, 1)
                        wait_first(po, zl_done, 2 * (past.t + 1))
                        for half in (0, 1):
                            for k in (0, 1):
                                po.indirect_dma_start(BUF, bass.IndirectOffsetOnAxis(ap=sloti[:, past.par, half, k:k + 1], axis=0),
                                                      zrow[:, past.par, half, :], None, bounds_check=SLOTS - 1,
                                                      oob_is_err=False).then_inc(scattered[past.par], 16)

            over_steps(po, step)

            def high_a(q, pc, k):
                wait_first(po, mul_done, q + 1)
                po.tensor_copy(act[:, pc, 0, k, :], a32[:, k % 2, :]).then_inc(a_hi, 1)

            def meta(c, pc):
                wait_first(po, first_done, 2 * c + 1)
                own = Order(meta_step, 6 * c)
                own(po.tensor_scalar(eq[:, 1, :], isfirst[:, pc, :], -1.0, 1.0, ALU.mult, ALU.add))
                own(po.tensor_tensor(eq[:, 2, :], isfirst[:, pc, :], rows[:, pc, :, META_W], ALU.mult))
                own(po.tensor_scalar(dest[:], eq[:, 1, :], float(N), None, ALU.mult))
                own(po.tensor_tensor(eq[:, 0, :], eq[:, 1, :], rows[:, pc, :, META_W + 1], ALU.mult))
                own(po.tensor_tensor(dest[:], dest[:], rows[:, pc, :, META_N], ALU.add))
                own(po.tensor_tensor(eq[:, 2, :], eq[:, 2, :], eq[:, 0, :], ALU.add))
                if not (isinstance(c, int) and c < 2):
                    wait_first(po, y_out[pc], 40 * c - 40 * pc)
                po.tensor_copy(desti[:, pc, :, 0], dest[:]).then_inc(meta_ready, 1)
                po.tensor_scalar(cw[:, pc, :], eq[:, 2, :], 1.0 / (W13S * W2S), None, ALU.mult).then_inc(meta_ready, 1)

            high_a(0, 0, 0)
            meta(0, 0)

            def chunk(c, pc, i, e, pe_, nxt, unit):
                high_a(4 * c + 1, pc, 1)
                high_a(4 * c + 2, pc, 0 + 2)
                high_a(4 * c + 3, pc, 3)
                if nxt is not None:
                    high_a(4 * c + 4, 1 - pc, 0)
                wait_first(po, y_ev, 3 * c + 3)
                wait_first(po, meta_ready, 2 * (c + 1))
                for m in range(5):
                    po.indirect_dma_start(Y, bass.IndirectOffsetOnAxis(ap=desti[:, pc, m, :], axis=0), yout[:, pc, m, :], None,
                                          bounds_check=2 * N - 1, oob_is_err=False).then_inc(y_out[pc], 16)
                if nxt is not None:
                    meta(c + 1, 1 - pc)

            for p in (0, 1):
                wait_first(po, zeros_out[p], 16 * (IMAGES // 2))
            over_chunks(po, chunk)


_INS = ["x", "L0_tok_W", "L0_tok_b", "L0_attn_ln_w", "L0_attn_W_qk", "L0_attn_W_o", "L0_attn_wte",
        "L0_ffn_gate_w", "L0_ffn_w13", "L0_ffn_w2", "L0_ffn_norm_w"]


def kernel(**inputs):
    import numpy as np
    import concourse.bacc as bacc
    from concourse import mybir as mb
    from concourse.bass_utils import run_bass_kernel_spmd

    nc = bacc.Bacc("TRN2", target_bir_lowering=False, num_devices=1)
    arrays, args = {}, []
    for name in _INS:
        a = np.ascontiguousarray(inputs[name])
        arrays[name] = a
        args.append(nc.dram_tensor(name, a.shape, mb.dt.from_np(a.dtype), kind="ExternalInput").ap())
    args.append(nc.dram_tensor("out", (IMAGES, TOK, E), mb.dt.float32, kind="ExternalOutput").ap())
    build(nc, *args)
    r = run_bass_kernel_spmd(nc, [arrays], core_ids=[0])
    return r.results[0]["out"]
```

```python
from contextlib import ExitStack

import concourse.bass as bass
from concourse import mybir

F32, F16, BF16 = mybir.dt.float32, mybir.dt.float16, mybir.dt.bfloat16
I32, U32 = mybir.dt.int32, mybir.dt.uint32
ALU, ACT, AX = mybir.AluOpType, mybir.ActivationFunctionType, mybir.AxisListType

IMAGES, CH, SIDE, PATCH = 64, 3, 224, 16
GRID = SIDE // PATCH
TOK = GRID * GRID
R = TOK // 2
E = 192
HEADS, PAIRS = 12, 6
VOCAB = 50257
N = IMAGES * TOK
EXPERTS, HID = 8, 512
CAP = -(-5 * 2 * N // (4 * EXPERTS))
SLOTS = EXPERTS * CAP
CHUNK = 5 * R
PER_EXPERT = CAP // CHUNK
CHUNKS = EXPERTS * PER_EXPERT
ROW = E + 4
META_N, META_SLOT, META_W = E, E + 1, E + 2
BIG = float(1 << 20)

QS = 64.0
PS = 2.0 ** 14
OS = 2.0 ** -5
WOS = 2.0 ** 8
ATT = 1.0 / (PS * OS * WOS)
W13S, W2S = 16.0, 16.0
SC = 1.0 / (QS * float(E) ** 0.5)
assert CAP % CHUNK == 0 and PER_EXPERT == 8

TOK_SLOTS = [5, 6, 7, 8, 9, 10, 11, 0, 1, 2, 3]
TOK_STEPS = [3, 2, 2, 2, 1, 1, 1, 1, 1, 1, 1]
WROWS = 14
WCHUNKS = VOCAB // 128 // WROWS
WREST = VOCAB - WCHUNKS * WROWS * 128
XCOLS = SIDE - 8


class At:

    def __init__(self, half, par):
        self.half, self.par, self.t = half, par, 2 * half + par

    def shift(self, k):
        p = self.par + k
        return At(self.half + p // 2, p % 2)


def head_at(at, h):
    return at.shift(h // HEADS), h % HEADS


def build(nc, x, tok_W, tok_b, ln_w, W_qk, W_o, wte, gate_w, w13, w2, norm_w, out):
    ctx = ExitStack()
    with ctx:
        def sb(name, shape, dt=F32):
            return ctx.enter_context(nc.sbuf_tensor(name, shape, dt))

        def sem(name):
            return ctx.enter_context(nc.semaphore(name))

        SUM = nc.dram_tensor("SUM", (N + CHUNK, E), F32).ap()
        BUF = nc.dram_tensor("BUF", (SLOTS, ROW), F32).ap()

        id32 = sb("id32", [128, 128])
        id16 = sb("id16", [128, 128], F16)
        idbf = sb("idbf", [R, R], BF16)
        maskbf = sb("maskbf", [R, R], BF16)
        before = sb("before", [R, R], F16)
        ones16 = sb("ones16", [R, R], F16)
        ones32 = sb("ones32", [128, R])
        halfneg = sb("halfneg", [R, 4])
        iota8 = sb("iota8", [R, EXPERTS])
        iotai = sb("iotai", [R, 16], I32)
        limit = sb("limit", [R, EXPERTS])
        base = sb("base", [R, EXPERTS])
        nreg = sb("nreg", [R, 2])
        tokid = sb("tokid", [R, 2])
        slotid = sb("slotid", [R, 5])
        empty = sb("empty", [R, 5, ROW])

        wtok = sb("wtok", [96, 8, E])
        btok = sb("btok", [R, E])
        lnw = sb("lnw", [R, E])
        avg = sb("avg", [R, E])
        q2 = sb("q2", [128, 2, HEADS])
        wo = sb("wo", [128, 2, 3 * PAIRS, E], F16)
        gateT = sb("gateT", [128, 2, EXPERTS])
        nwT = sb("nwT", [128, 2, EXPERTS])
        stream = sb("stream", [128, 3, WROWS * E])
        wpart = sb("wpart", [128, 2, E])
        raw = sb("raw", [128, 2304])
        raw2 = sb("raw2", [64, 2304])
        small = sb("small", [12, 6, 256])

        X = sb("X", [128, GRID * SIDE + 2 * 8 * TOK])
        ximg = X[0:96, 0:GRID * SIDE].rearrange("p (m w) -> p m w", w=SIDE)
        xtok = X[0:96, GRID * SIDE:].rearrange("p (c n q) -> p c n q", c=2, q=8)
        hbuf = sb("hbuf", [R, 2, 2, E])
        st1 = sb("st1", [R, 2, 6])
        mv1 = sb("mv1", [R, 2, 2])
        pw1 = sb("pw1", [R, 6, 2])
        xn = sb("xn", [R, 2, 256])
        V32 = sb("V32", [R, 2, E])
        V = sb("V", [R, 2, 2, 2, 320], F16)
        xT = sb("xT", [128, 2, 2, TOK])
        XT = sb("XT", [128, 2, 2, 2, TOK], F16)
        L = sb("L", [128, 3, 3, TOK], F16)
        P = sb("P", [R, 4, 3 * R])
        mx = sb("mx", [R, 2, 2])
        nm = sb("nm", [R, 2, 2])
        sums = sb("sums", [R, 4, 2])
        rinv = sb("rinv", [R, 4, 2])
        PT = sb("PT", [R, 2, 2, 2, 3 * R], F16)
        OT = sb("OT", [128, 2, 2, 3, TOK], F16)
        h2 = sb("h2", [R, 2, 2, E])
        st3 = sb("st3", [R, 2, 6])
        mv3 = sb("mv3", [R, 2, 2])
        pw3 = sb("pw3", [R, 7, 2])
        xf = sb("xf", [R, 2, 2, E])
        z32 = sb("z32", [R, 2, E])
        zrow = sb("zrow", [R, 2, 2, ROW])
        xfT = sb("xfT", [128, 2, TOK])
        top = sb("top", [R, 2, 8])
        topi = sb("topi", [R, 2, 8], U32)
        topf = sb("topf", [R, 2, 2])
        dif = sb("dif", [R, 2])
        edif = sb("edif", [R, 2])
        eden = sb("eden", [R, 2])
        wk = sb("wk", [R, 2, 2])
        oh = sb("oh", [R, 2, 2, EXPERTS])
        both = sb("both", [R, 2, EXPERTS], F16)
        place = sb("place", [R, 2, EXPERTS])
        over = sb("over", [R, 2, EXPERTS])
        picked = sb("picked", [R, 2, 2, EXPERTS])
        slot = sb("slot", [R, 2, 2])
        sloti = sb("sloti", [R, 2, 2, 2], I32)
        kept = sb("kept", [R, 2, 2])
        kw = sb("kw", [R, 2])
        hout = sb("hout", [R, 2, 2, E])

        rows = sb("rows", [R, 2, 5, ROW])
        zT = sb("zT", [128, 2, 3, CHUNK], F16)
        w13t = sb("w13t", [128, 2, 4, 2 * HID], F16)
        w2t = sb("w2t", [128, 2, 2, 4, E], F16)
        r13 = sb("r13", [128, 2, 256])
        r2 = sb("r2", [96, 2, 128])
        sg = raw[:, 0:2 * CHUNK].rearrange("p (k s) -> p k s", k=2)
        a32 = raw[:, 2 * CHUNK:4 * CHUNK].rearrange("p (k s) -> p k s", k=2)
        act = X[:, 0:8 * CHUNK].bitcast(F16).rearrange("p (c n k s) -> p c n k s", c=2, n=2, k=4)
        yout = stream[:].rearrange("p a b -> p (a b)")[0:R, 0:10 * E].rearrange("p (c r e) -> p c r e", c=2, r=5)
        isfirst = sb("isfirst", [R, 2, 5])
        eq = sb("eq", [R, 3, 5])
        desti = sb("desti", [R, 2, 5, 1], I32)
        cw = sb("cw", [R, 2, 5])

        banks = ctx.enter_context(nc.psum_tensor("banks", [128, 8, 512], F32))
        pT, pOA, pOB, pPJ, pSTG, pACC = (banks[:, b, :] for b in range(2, 8))
        LG, CU = 400, 416
        zbank = banks[:, 4:6, :].rearrange("p b n -> p (b n)").bitcast(F16)
        prep = banks[:, 5, 256:512]

        c_ready = sem("c_ready")
        w_in = [sem(f"w_in{i}") for i in range(3)]
        w_red = sem("w_red")
        w_sum = sem("w_sum")
        raw_in = sem("raw_in")
        raw2_in = sem("raw2_in")
        wo_in = sem("wo_in")
        small_in = sem("small_in")
        bc_in = sem("bc_in")
        pt_done = sem("pt_done")
        pt_act = sem("pt_act")
        pt_dve = sem("pt_dve")
        empty_out = sem("empty_out")
        x_in = sem("x_in")
        x_al = sem("x_al")
        tok_done = sem("tok_done")
        h_done = sem("h_done")
        pre_dve = sem("pre_dve")
        pre_pool = sem("pre_pool")
        stat1 = sem("stat1")
        r1_done = sem("r1_done")
        zs_done = sem("zs_done")
        pool_order = sem("pool_order")
        fill_ready = sem("fill_ready")
        xn_done = sem("xn_done")
        hcopy_done = sem("hcopy_done")
        dup_done = sem("dup_done")
        v32_done = sem("v32_done")
        vh_done = sem("vh_done")
        vl_done = sem("vl_done")
        v_ready = sem("v_ready")
        xtp_done = sem("xtp_done")
        xt32_done = sem("xt32_done")
        xth_done = sem("xth_done")
        xtl_done = sem("xtl_done")
        lhi = sem("lhi")
        l_ready = sem("l_ready")
        s_done = sem("s_done")
        max_done = sem("max_done")
        nm_ready = sem("nm_ready")
        exp_done = sem("exp_done")
        r_ready = sem("r_ready")
        n_done = sem("n_done")
        t_done = sem("t_done")
        pt_hi = sem("pt_hi")
        pt_lo = sem("pt_lo")
        ot_done = sem("ot_done")
        ot_hi = sem("ot_hi")
        ot_lo = sem("ot_lo")
        pj_done = sem("pj_done")
        h2_done = sem("h2_done")
        bn3 = sem("bn3")
        stat3 = sem("stat3")
        post_pool = sem("post_pool")
        r3_done = sem("r3_done")
        xf_done = sem("xf_done")
        z32_done = sem("z32_done")
        zh_done = sem("zh_done")
        zl_done = sem("zl_done")
        ftp_done = sem("ftp_done")
        xfT_done = sem("xfT_done")
        lg_done = sem("lg_done")
        route = sem("route")
        e_done = sem("e_done")
        both_done = sem("both_done")
        cu_done = sem("cu_done")
        slot_done = sem("slot_done")
        meta_done = sem("meta_done")
        scattered = [sem(f"scattered{i}") for i in range(2)]
        hout_done = sem("hout_done")
        hout_out = [sem(f"hout_out{i}") for i in range(2)]

        rows_in = [sem(f"rows_in{i}") for i in range(2)]
        r13_in = [sem(f"r13_in{i}") for i in range(2)]
        ft_done = sem("ft_done")
        zt_a = sem("zt_a")
        zt_b = sem("zt_b")
        gu_done = sem("gu_done")
        silu_done = sem("silu_done")
        mul_done = sem("mul_done")
        a_hi = sem("a_hi")
        a_lo = sem("a_lo")
        u13_done = sem("u13_done")
        u13_hi = sem("u13_hi")
        u13_lo = sem("u13_lo")
        u2_done = sem("u2_done")
        u2_hi = sem("u2_hi")
        u2_lo = sem("u2_lo")
        y_done = sem("y_done")
        y_ev = sem("y_ev")
        first_done = sem("first_done")
        meta_step = sem("meta_step")
        meta_ready = sem("meta_ready")
        y_out = [sem(f"y_out{i}") for i in range(2)]
        out_done = sem("out_done")

        block = ctx.enter_context(nc.Block())

        def heads(at, h):
            a, k = head_at(at, h)
            return HEADS * a.t + k + 1

        def pairs(at, q):
            a = at.shift(q // PAIRS)
            return PAIRS * a.t + q % PAIRS + 1

        def wait(eng, s, n):
            if not (isinstance(n, int) and n <= 0):
                eng.wait_ge(s, n)

        def wait_first(eng, s, n):
            if not isinstance(n, int):
                n = eng.to_reg(n)
                eng.wait_ge(c_ready, 1)
            wait(eng, s, n)

        def over_steps(eng, step):
            step(At(-1, 1), True, False, False, False)
            step(At(0, 0), True, True, False, False)
            step(At(0, 1), True, True, True, False)
            last = IMAGES // 2 - 1
            with eng.Fori(1, last - 1) as j:
                for par in (0, 1):
                    step(At(j, par), True, True, True, True)
            step(At(last - 1, 0), True, True, True, True)
            step(At(last - 1, 1), True, True, True, True)
            step(At(last, 0), True, True, True, True)
            step(At(last, 1), False, True, True, True)
            step(At(last + 1, 0), False, False, True, True)
            step(At(last + 1, 1), False, False, False, True)

        def over_chunks(eng, chunk):
            def expert(e, pe, last):
                with eng.Fori(0, PER_EXPERT // 2 - 1) as i:
                    for pc in (0, 1):
                        chunk(e * PER_EXPERT + 2 * i + pc, pc, i, e, pe, pe, not last)
                i = PER_EXPERT // 2 - 1
                for pc in (0, 1):
                    nxt = pe if pc == 0 else (None if last else 1 - pe)
                    chunk(e * PER_EXPERT + 2 * i + pc, pc, i, e, pe, nxt, not last)

            with eng.Fori(0, EXPERTS // 2 - 1) as ep:
                expert(2 * ep, 0, False)
                expert(2 * ep + 1, 1, False)
            expert(EXPERTS - 2, 0, False)
            expert(EXPERTS - 1, 1, True)

        @block.sync
        def _(sp):
            def load_x(at):
                wait_first(sp, x_al, 9 * at.t)
                for half in (0, 1):
                    src = x[bass.ds(at.t, 1), :, :, 8 * half:8 * half + XCOLS].rearrange("o c h w -> (o c h) w")
                    src = src.rearrange("(m g r) w -> g r m w", g=3, r=PATCH)
                    for g in range(3):
                        sp.dma_start(X[32 * g + half:32 * g + 32:2, 0:GRID * SIDE].rearrange("p (m w) -> p m w", w=SIDE)[:, :, 0:XCOLS],
                                     src[g]).then_inc(x_in, 16)

            def load_wte(k):
                if k >= 3:
                    sp.wait_ge(w_red, k - 2)
                n = WROWS * 128
                sp.dma_start(stream[:, k % 3, :], wte[k * n:(k + 1) * n, :].rearrange("(p r) e -> p (r e)", p=128)
                             ).then_inc(w_in[k % 3], 16)

            def load_unit(v, pc, i, e):
                if not (isinstance(v, int) and v < 2):
                    wait_first(sp, u13_done, v - 1)
                    wait_first(sp, u2_done, v - 1)
                rows13 = w13[bass.ds(e, 1), bass.ds((2 * i + pc) * 128, 128), :]
                sp.dma_start(r13[:, pc, 0:E], rows13.rearrange("o p e -> (o p) e")).then_inc(r13_in[pc], 16)
                rows13 = w13[bass.ds(e, 1), bass.ds((2 * i + pc) * 128, 128), 128:E]
                sp.dma_start(r13[:, pc, E:256], rows13.rearrange("o p e -> (o p) e")).then_inc(r13_in[pc], 16)
                block2 = w2[bass.ds(e, 1), pc * 96:pc * 96 + 96, bass.ds(i * 128, 128)]
                sp.dma_start(r2[:, pc, :], block2.rearrange("o p h -> (o p) h")).then_inc(r13_in[pc], 16)

            sp.dma_start(small[0:EXPERTS, 0, 0:E], gate_w).then_inc(small_in, 16)
            sp.dma_start(small[0:EXPERTS, 1, 0:E], norm_w).then_inc(small_in, 16)
            sp.dma_start(small[0:EXPERTS, 1, E:256], norm_w[:, 128:E]).then_inc(small_in, 16)
            sp.dma_start(small[0:HEADS, 2, 0:E], W_qk).then_inc(small_in, 16)
            sp.dma_start(small[0:HEADS, 2, E:256], W_qk[:, 128:E]).then_inc(small_in, 16)
            sp.dma_start(btok[:], tok_b.rearrange("(o e) -> o e", o=1).to_broadcast([R, E])).then_inc(bc_in, 16)
            sp.dma_start(lnw[:], ln_w.rearrange("(o e) -> o e", o=1).to_broadcast([R, E])).then_inc(bc_in, 16)
            sp.dma_start(raw[:, 0:768], tok_W[0:128, :]).then_inc(raw_in, 16)
            sp.dma_start(raw2[:, 0:768], tok_W[128:E, :]).then_inc(raw2_in, 16)
            load_x(At(0, 0))
            load_wte(0)
            load_wte(1)
            load_wte(2)
            sp.wait_ge(pt_done, 17)
            for r, lo, hi in ((raw, 0, 128), (raw2, 128, E)):
                src = W_o[lo:hi, :].rearrange("p (h e) -> p h e", h=HEADS)
                for col, a, b in ((0, 0, 128), (HEADS * 128, 128, E)):
                    sp.dma_start(r[:, col:col + HEADS * (b - a)].rearrange("p (h e) -> p h e", h=HEADS), src[:, :, a:b]
                                 ).then_inc(wo_in, 16)
            for k in range(3, WCHUNKS):
                v = (k - PAIRS - 3) // 2
                if (k - PAIRS) % 2 and 0 <= v < PER_EXPERT:
                    load_unit(v, v % 2, v // 2, 0)
                load_wte(k)
                if k == WCHUNKS // 2:
                    load_x(At(0, 1))
            sp.wait_ge(w_red, WCHUNKS - 2)
            sp.dma_start(stream[0:WREST, WCHUNKS % 3, 0:E], wte[WCHUNKS * WROWS * 128:VOCAB, :]).then_inc(w_in[WCHUNKS % 3], 16)
            sp.wait_ge(fill_ready, 1)

            def empty_slots(first, last):
                for k in range(first, last):
                    sp.dma_start(BUF[k * CHUNK:(k + 1) * CHUNK, :].rearrange("(p r) c -> p r c", p=R), empty[:]
                                 ).then_inc(empty_out, 16)

            def step(at, nxt, main, prev, prev2):
                if nxt:
                    a = at.shift(3)
                    if not (isinstance(a.t, int) and a.t >= IMAGES):
                        load_x(a)
                if isinstance(at.t, int) and at.t < 2:
                    third = -(-CHUNKS // 3)
                    empty_slots((at.t + 1) * third, min((at.t + 2) * third, CHUNKS))
                if prev2:
                    a = at.shift(-2)
                    wait_first(sp, hout_done, 2 * (a.t + 1))
                    sp.dma_start(SUM[bass.ds(a.t * TOK, TOK), :].rearrange("(h p) e -> p h e", p=R),
                                 hout[:, a.par]).then_inc(hout_out[a.par], 16)

            over_steps(sp, step)

            def load_rows(c, pc):
                sp.dma_start(rows[:, pc], BUF[bass.ds(c * CHUNK, CHUNK), :].rearrange("(p r) c -> p r c", p=R)
                             ).then_inc(rows_in[pc], 16)

            for p in (0, 1):
                sp.wait_ge(scattered[p], 64 * (IMAGES // 2))
            load_rows(0, 0)

            def chunk(c, pc, i, e, pe, nxt, unit):
                if nxt is not None:
                    wait_first(sp, ft_done, c)
                    wait_first(sp, meta_ready, 2 * c)
                    load_rows(c + 1, 1 - pc)
                if unit:
                    load_unit(c + PER_EXPERT, pc, i, e + 1)

            over_chunks(sp, chunk)

            for p in (0, 1):
                sp.wait_ge(y_out[p], 80 * (CHUNKS // 2))
            pieces = 8
            rows_out = out.rearrange("b t e -> (b t) e")
            for k in range(pieces):
                part = slice(k * N // pieces, (k + 1) * N // pieces)
                sp.dma_start(rows_out[part, :].rearrange("(q r) e -> q (r e)", q=16),
                             SUM[part, :].rearrange("(q r) e -> q (r e)", q=16)).then_inc(out_done, 16)
            sp.wait_ge(out_done, 16 * pieces)

        @block.tensor
        def _(pe):
            pe.wait_ge(c_ready, 1)
            pe.wait_ge(small_in, 80)
            pe.transpose(pT[:, 0:8], small[0:8, 0, 0:128], id32[0:8, 0:8])
            pe.transpose(pT[0:64, 8:16], small[0:8, 0, 128:192], id32[0:8, 0:8])
            pe.transpose(pT[:, 16:24], small[0:8, 1, 0:128], id32[0:8, 0:8])
            pe.transpose(pT[:, 24:32], small[0:8, 1, 128:256], id32[0:8, 0:8])
            pe.transpose(pT[:, 32:44], small[0:12, 2, 0:128], id32[0:12, 0:12])
            pe.transpose(pT[:, 44:56], small[0:12, 2, 128:256], id32[0:12, 0:12]).then_inc(pt_done, 1)
            pe.wait_ge(raw_in, 16)
            pe.wait_ge(raw2_in, 16)
            for q in range(8):
                if q >= 2:
                    pe.wait_ge(pt_act, 2 + q - 1)
                bank = banks[0:96, q % 2, 0:E]
                sel = raw[:, 0:768].rearrange("p (k q) -> p k q", q=8)[:, :, q]
                sel2 = raw2[:, 0:768].rearrange("p (k q) -> p k q", q=8)[:, :, q]
                pe.transpose(bank[:, 0:128], sel, id32[:]).then_inc(pt_done, 1)
                pe.transpose(bank[:, 128:E], sel2, id32[0:64, 0:64]).then_inc(pt_done, 1)
            def wte_sum(k):
                pe.wait_ge(w_red, k + 1)
                pe.matmul(pSTG[0:R, 0:E], ones32[:], wpart[:, k % 2, :], start=(k == 0), stop=False).then_inc(w_sum, 1)

            pe.wait_ge(wo_in, 64)
            for q in range(PAIRS):
                for k in range(3):
                    n = 3 * q + k
                    pe.wait_ge(pt_dve, n) if n >= 2 else pe.wait_ge(pt_act, 10)
                    bank = banks[:, n % 2, 0:E]
                    for r, lo, hi in ((raw, 0, 128), (raw2, 128, E)):
                        part = 2 * q + k if k < 2 else HEADS + q
                        mm = pe.transpose(bank[:, lo:hi], r[:, part * 128:part * 128 + 128], id32[0:hi - lo, 0:hi - lo])
                    mm.then_inc(pt_done, 1)
                wte_sum(q)

            def gu(c_count, pc, pe_, k):
                if not (isinstance(c_count, int) and 4 * c_count + k < 2):
                    wait(pe, mul_done, 4 * c_count + k - 1)
                for u in (0, 1):
                    o = banks[:, 2 * (k % 2) + u, 0:CHUNK]
                    col = u * HID + k * 128
                    for n, (w, z) in enumerate(((0, 0), (0, 1), (1, 0), (2, 2), (3, 2))):
                        mm = pe.matmul(o, w13t[:, pe_, w, col:col + 128], zT[:, pc, z, :], start=(n == 0), stop=(n == 4))
                mm.then_inc(gu_done, 1)

            def ft(c, pc):
                wait(pe, rows_in[pc], 16 * ((c - pc) // 2 + 1) if isinstance(c, int) else c * 8 + (16 - 8 * pc))
                if not (isinstance(c, int) and c == 0):
                    wait(pe, zt_a, c)
                    wait(pe, zt_b, c)
                for m in range(5):
                    r16 = rows[:, pc, m, 0:E].bitcast(F16)
                    for n, col in enumerate((0, 256, 128)):
                        mm = pe.transpose(zbank[:, 512 * n + R * m:512 * n + R * m + R], r16[:, col:col + 128], id16[0:R, 0:R])
                mm.then_inc(ft_done, 1)

            def unit13(v, pc):
                wait(pe, r13_in[pc], 48 * ((v - pc) // 2 + 1) if isinstance(v, int) else v * 24 + (48 - 24 * pc))
                if not (isinstance(v, int) and v == 0):
                    wait(pe, u2_lo, v)
                pe.transpose(prep[:, 0:128], r13[:, pc, 0:128], id32[:])
                pe.transpose(prep[:, 128:256], r13[:, pc, 128:256], id32[:]).then_inc(u13_done, 1)

            def unit2(v, pc):
                wait(pe, u13_lo, 2 * v + 2)
                pe.transpose(prep[:, 0:96], r2[:, pc, :], id32[0:96, 0:96]).then_inc(u2_done, 1)

            for k in range(PAIRS, WCHUNKS):
                v = (k - PAIRS) // 2
                if (k - PAIRS) % 2 == 0 and v < PER_EXPERT:
                    unit13(v, v % 2)
                    unit2(v, v % 2)
                wte_sum(k)
            pe.wait_ge(w_in[WCHUNKS % 3], 16 * (WCHUNKS // 3 + 1))
            pe.matmul(pSTG[0:R, 0:E], ones32[0:WREST, :], stream[0:WREST, WCHUNKS % 3, 0:E], start=False, stop=True).then_inc(w_sum, 1)

            def tok(at, s):
                i = TOK_SLOTS.index(s)
                if i == 0:
                    pe.wait_ge(x_al, 9 * (at.t + 1))
                    wait(pe, h_done, at.t)
                first = sum(TOK_STEPS[:i])
                for n in range(first, first + TOK_STEPS[i]):
                    half, q = n // 8, n % 8
                    mm = pe.matmul(pACC[0:R, half * E:half * E + E], xtok[:, at.par, R * half:R * half + R, q],
                                   wtok[:, q, :], start=(q == 0), stop=(q == 7))
                if i == len(TOK_STEPS) - 1:
                    mm.then_inc(tok_done, 1)

            def scores(at, h):
                pe.wait_ge(l_ready, heads(at, h))
                if h == 0:
                    pe.wait_ge(xth_done, at.t + 1)
                wait(pe, exp_done, 2 * heads(at, h - 2))
                par = h % 2
                for half in (0, 1):
                    cols = R * (half + 1)
                    o = banks[0:R, par, R * half:R * half + cols]
                    s = slice(R * half, R * half + R)
                    Lh = L[:, h % 3]
                    terms = ((0, 0, 0), (1, 0, 0), (0, 1, 0), (2, 0, 1), (2, 1, 1))
                    for n, (lp, part, ab) in enumerate(terms):
                        pe.matmul(o, Lh[:, lp, s], XT[:, at.par, part, ab, 0:cols], start=(n == 0), stop=False)
                    mm = pe.matmul(o[:, cols - R:cols], idbf[:], maskbf[:], start=False, stop=True)
                mm.then_inc(s_done, 1)

            def turn(at, h):
                pe.wait_ge(n_done, 2 * heads(at, h))
                wait(pe, pt_lo, heads(at, h - 1))
                for k in range(3):
                    mm = pe.transpose(pT[0:R, R * k:R * k + R], P[:, h % 4, R * k:R * k + R], id32[0:R, 0:R])
                mm.then_inc(t_done, 1)

            def sum_v(at, q):
                pe.wait_ge(pt_lo, heads(at, 2 * q + 1))
                wait(pe, ot_lo, 2 * pairs(at, q - 1))
                if q == 0:
                    pe.wait_ge(v_ready, 2 * (at.t + 1))
                p = q % 2
                terms = ((0, 0), (1, 0), (0, 1))
                oA = pOA[:, 0:2 * TOK].rearrange("p (h s) -> p h s", h=2)
                for n, (vp, pp) in enumerate(terms):
                    pe.matmul(oA, V[:, at.par, vp, 0, 0:128], PT[:, p, pp, :, 0:TOK], start=(n == 0), stop=False)
                for n, (vp, pp) in enumerate(terms):
                    pe.matmul(oA[:, :, R:TOK], V[:, at.par, vp, 1, 0:128], PT[:, p, pp, :, TOK:3 * R],
                              start=False, stop=(n == 2))
                for hd in (0, 1):
                    c = 128 + 64 * hd
                    for n, (vp, pp) in enumerate(terms):
                        pe.matmul(pOB[:, 0:TOK], V[:, at.par, vp, 0, c:c + 128], PT[:, p, pp, hd, 0:TOK],
                                  start=(hd == 0 and n == 0), stop=False)
                    for n, (vp, pp) in enumerate(terms):
                        mm = pe.matmul(pOB[:, R:TOK], V[:, at.par, vp, 1, c:c + 128], PT[:, p, pp, hd, TOK:3 * R],
                                       start=False, stop=(hd == 1 and n == 2))
                mm.then_inc(ot_done, 1)

            def project(at, q):
                pe.wait_ge(ot_lo, 2 * pairs(at, q))
                if q == 0:
                    wait(pe, h2_done, at.t)
                p = q % 2
                for half in (0, 1):
                    o = pPJ[0:R, E * half:E * half + E]
                    for k in range(3):
                        for op, wp in ((0, 0), (1, 0), (0, 1)):
                            mm = pe.matmul(o, OT[:, p, op, k, R * half:R * half + R], wo[:, wp, 3 * q + k, :],
                                           start=(q == 0 and half == 0 and k == 0 and (op, wp) == (0, 0)),
                                           stop=(q == PAIRS - 1 and k == 2 and wp == 1), skip_group_check=True)
                if q == PAIRS - 1:
                    mm.then_inc(pj_done, 1)

            def step(at, nxt, main, prev, prev2):
                for s in range(HEADS):
                    a, h = head_at(at, s - 4)
                    if (main if s >= 4 else prev):
                        turn(a, h)
                    q = (s - 6) // 2
                    if s % 2 == 0 and (main if q >= 0 else prev):
                        sum_v(at.shift(q // PAIRS), q % PAIRS)
                    if main:
                        scores(at, s)
                    if nxt and s == 9:
                        a = at.shift(1)
                        pe.wait_ge(dup_done, a.t + 1)
                        wait(pe, xfT_done, 2 * (a.t - 2))
                        if prev2:
                            pe.wait_ge(route, 15 * at.shift(-2).t + 14)
                        for ab in (0, 1):
                            for half in (0, 1):
                                c = ab * TOK + half * R
                                mm = pe.transpose(pSTG[:, c:c + R], xn[:, half, 128 * ab:128 * ab + 128], id32[0:R, 0:R])
                        mm.then_inc(xtp_done, 1)
                    q = (s - 7) // 2
                    if s % 2 and (main if q >= 0 else prev):
                        project(at.shift(q // PAIRS), q % PAIRS)
                    if nxt and s < 4:
                        tok(at.shift(1), s)
                    if nxt and s > 4 and not (isinstance(at.t, int) and at.t + 2 >= IMAGES):
                        tok(at.shift(2), s)
                    if prev2 and s == 5:
                        a = at.shift(-2)
                        pe.wait_ge(both_done, a.t + 1)
                        pe.matmul(pSTG[0:R, CU:CU + 8], before[:], both[:, 0, :], start=True, stop=True)
                        pe.matmul(pSTG[0:R, CU + 8:CU + 16], before[:], both[:, 1, :], start=True, stop=False)
                        pe.matmul(pSTG[0:R, CU + 8:CU + 16], ones16[:], both[:, 0, :], start=False, stop=True)
                        pe.matmul(pSTG[0:R, CU + 16:CU + 24], ones16[:], both[:, 0, :], start=True, stop=False)
                        pe.matmul(pSTG[0:R, CU + 16:CU + 24], ones16[:], both[:, 1, :], start=False, stop=True).then_inc(cu_done, 1)
                    if prev and s == 10:
                        a = at.shift(-1)
                        pe.wait_ge(xf_done, 2 * (a.t + 1))
                        if nxt:
                            pe.wait_ge(xtl_done, at.t + 2)
                        elif prev2:
                            pe.wait_ge(route, 15 * at.shift(-2).t + 14)
                        for half in (0, 1):
                            pe.transpose(pSTG[:, half * R:half * R + R], xf[:, a.par, half, 0:128], id32[0:R, 0:R])
                        for half in (0, 1):
                            c = TOK + half * R
                            mm = pe.transpose(pSTG[0:64, c:c + R], xf[:, a.par, half, 128:E], id32[0:R, 0:R])
                        mm.then_inc(ftp_done, 1)
                    if prev2 and s == 0:
                        a = at.shift(-2)
                        pe.wait_ge(xfT_done, 2 * (a.t + 1))
                        for half in (0, 1):
                            o = pSTG[0:R, LG + 8 * half:LG + 8 * half + 8]
                            hs = slice(half * R, half * R + R)
                            pe.matmul(o, xfT[:, 0, hs], gateT[:, 0, :], start=True, stop=False)
                            mm = pe.matmul(o, xfT[0:64, 1, hs], gateT[0:64, 1, :], start=False, stop=True)
                        mm.then_inc(lg_done, 1)

            pe.wait_ge(u2_lo, PER_EXPERT)
            for s in TOK_SLOTS[:-4]:
                tok(At(0, 0), s)
            over_steps(pe, step)

            for s_, n in ((exp_done, 2 * HEADS), (pt_lo, HEADS), (ot_lo, 2 * PAIRS), (h2_done, 1), (h_done, 1)):
                pe.wait_ge(s_, n * IMAGES)
            pe.wait_ge(route, 15 * IMAGES + 1)
            ft(0, 0)
            pe.wait_ge(zt_a, 1)
            pe.wait_ge(zt_b, 1)
            pe.wait_ge(u13_lo, 2 * PER_EXPERT)
            pe.wait_ge(u13_hi, 2 * PER_EXPERT)
            gu(0, 0, 0, 0)

            def rows_y(c, pc, pe_):
                pe.wait_ge(a_lo, 4 * c + 3)
                for u, tiles in enumerate(((0, 1), (2, 3), (4,))):
                    pe.wait_ge(y_ev, 3 * c + max(u - 1, 0))
                    for k in range(4):
                        if u == 0 and k == 3:
                            pe.wait_ge(a_lo, 4 * c + 4)
                        for n, m in enumerate(tiles):
                            o = banks[0:R, 6 + (pc + u) % 2, E * n:E * n + E]
                            for ap, wp in ((0, 0), (1, 0), (0, 1)):
                                mm = pe.matmul(o, act[:, pc, ap, k, R * m:R * m + R], w2t[:, pe_, wp, k, :],
                                               start=(n == 0 and k == 0 and ap == 0 and wp == 0),
                                               stop=(k == 3 and wp == 1), skip_group_check=True)
                    mm.then_inc(y_done, 1)

            def chunk(c, pc, i, e, pe_, nxt, unit):
                gu(c, pc, pe_, 1)
                if unit:
                    pe.wait_ge(u2_lo, c + PER_EXPERT)
                if nxt is not None:
                    ft(c + 1, 1 - pc)
                gu(c, pc, pe_, 2)
                if unit:
                    pe.wait_ge(zt_b, c + 2)
                    unit13(c + PER_EXPERT, pc)
                gu(c, pc, pe_, 3)
                if unit:
                    unit2(c + PER_EXPERT, pc)
                if nxt is not None:
                    pe.wait_ge(zt_a, c + 2)
                    pe.wait_ge(zt_b, c + 2)
                    if nxt != pe_:
                        pe.wait_ge(u13_lo, 2 * (c + PER_EXPERT + 1))
                        pe.wait_ge(u2_lo, c + PER_EXPERT + 1)
                    gu(c + 1, 1 - pc, nxt, 0)
                rows_y(c, pc, pe_)

            over_chunks(pe, chunk)

        @block.scalar
        def _(sc):
            sc.wait_ge(pt_done, 1)
            sc.wait_ge(route, 1)
            sc.activation(gateT[:, 0, :], pT[:, 0:8], ACT.Copy).then_inc(pt_act, 1)
            sc.activation(gateT[0:64, 1, :], pT[0:64, 8:16], ACT.Copy)
            sc.activation(nwT[:], pT[:, 16:32].rearrange("p (a b) -> p a b", a=2), ACT.Copy, scale=W13S).then_inc(pt_act, 1)
            for q in range(8):
                sc.wait_ge(pt_done, 3 + 2 * q)
                sc.activation(wtok[:, q, :], banks[0:96, q % 2, 0:E], ACT.Copy).then_inc(pt_act, 1)
            for n in range(3 * PAIRS):
                sc.wait_ge(pt_done, 18 + n)
                sc.activation(wo[:, 0, n, :], banks[:, n % 2, 0:E], ACT.Copy, scale=WOS).then_inc(pt_act, 1)
            def unit13(v, pe_, blk, e):
                wait_first(sc, u13_done, v + 1)
                for ab in (0, 1):
                    sc.activation(w13t[:, pe_, 2 * ab, bass.ds(blk * 128, 128)], prep[:, 128 * ab:128 * ab + 128],
                                  ACT.Copy, scale=nwT[:, ab, bass.ds(e, 1)]).then_inc(u13_hi, 1)

            def unit2(v, pc, pe_, i):
                sc.wait_ge(u2_done, v + 1)
                sc.activation(w2t[:, pe_, 0, bass.ds(i, 1), 96 * pc:96 * pc + 96].rearrange("p o d -> p (o d)"), prep[:, 0:96],
                              ACT.Copy, scale=W2S).then_inc(u2_hi, 1)

            def align(at, n):
                j, g = n // 3, n % 3
                lo, hi = -(-(GRID * g - j) // 3), (GRID * g + GRID - 1 - j) // 3 + 1
                if n == 0:
                    sc.wait_ge(x_in, 96 * (at.t + 1))
                    wait(sc, tok_done, at.t - 1)
                col = PATCH * (3 * lo + j - GRID * g)
                src = ximg[32 * g:32 * g + 32, :, col:col + 3 * PATCH * (hi - lo - 1) + 8]
                src = bass.AP(src.tensor, src.offset, [*src.ap[:2], [3 * PATCH, hi - lo], [1, 8]])
                dst = xtok[32 * j:32 * j + 32, at.par].rearrange("p (m i) q -> p m i q", i=GRID)[:, :, lo:hi, :]
                sc.activation(dst, src, ACT.Copy).then_inc(x_al, 1)

            for n in range(9):
                align(At(0, 0), n)
            for v in range(PER_EXPERT):
                unit13(v, 0, v, 0)
                unit2(v, v % 2, 0, v // 2)
            for n in range(9):
                align(At(0, 1), n)
            sc.wait_ge(w_sum, WCHUNKS + 1)
            sc.activation(avg[:], pSTG[0:R, 0:E], ACT.Copy, scale=1.0 / VOCAB).then_inc(pt_act, 1)

            sc.wait_ge(pt_dve, 1)

            def high_l(at, h):
                if h == 0:
                    sc.wait_ge(xt32_done, at.t + 1)
                wait(sc, s_done, heads(at, h - 3))
                for k, ab in ((0, 0), (2, 1)):
                    sc.activation(L[:, h % 3, k, :], xT[:, at.par, ab, :], ACT.Copy, scale=q2[:, ab, h:h + 1]).then_inc(lhi, 1)

            def turned(at, k, there):
                if there:
                    a, h = head_at(at, k)
                    sc.wait_ge(t_done, heads(a, h))
                    sc.activation(PT[:, (h // 2) % 2, 0, h % 2, :], pT[0:R, 0:3 * R], ACT.Copy).then_inc(pt_hi, 1)

            def step(at, nxt, main, prev, prev2):
                for s in range(HEADS):
                    if (main if s < HEADS - 1 else nxt):
                        high_l(*head_at(at, s + 1))
                    turned(at, s - 4, main if s >= 4 else prev)
                    a, h = head_at(at, s - 1)
                    if (main if s >= 1 else prev):
                        sc.wait_ge(nm_ready, heads(a, h))
                        for half in (0, 1):
                            cols = slice(R * half, R * half + R * (half + 1))
                            sc.activation(P[:, h % 4, cols], banks[0:R, h % 2, cols], ACT.Exp, bias=nm[:, h % 2, half:half + 1],
                                          scale=SC, accum_out=sums[:, h % 4, half:half + 1]).then_inc(exp_done, 1)
                    q = (s - 6) // 2
                    if s % 2 == 0 and (main if q >= 0 else prev):
                        a, k = at.shift(q // PAIRS), q % PAIRS
                        sc.wait_ge(ot_done, pairs(a, k))
                        sc.activation(OT[:, k % 2, 0, 0:2, :], pOA[:, 0:2 * TOK].rearrange("p (h s) -> p h s", h=2),
                                      ACT.Copy, scale=OS).then_inc(ot_hi, 1)
                        sc.activation(OT[:, k % 2, 0, 2, :], pOB[:, 0:TOK], ACT.Copy, scale=OS).then_inc(ot_hi, 1)
                    if nxt and s >= 3:
                        a = at.shift(3)
                        if not (isinstance(a.t, int) and a.t >= IMAGES):
                            align(a, s - 3)
                    if prev2 and s == 2:
                        a = at.shift(-2)
                        sc.wait_ge(route, 15 * a.t + 6)
                        sc.activation(edif[:], dif[:], ACT.Exp).then_inc(e_done, 1)
                    if nxt and s == 9:
                        a = at.shift(1)
                        sc.wait_ge(xtp_done, a.t + 1)
                        stg = pSTG[:, 0:2 * TOK].rearrange("p (a s) -> p a s", a=2)
                        sc.activation(xT[:, a.par], stg, ACT.Copy).then_inc(xt32_done, 1)
                        sc.activation(XT[:, a.par, 0], stg, ACT.Copy).then_inc(xth_done, 1)
                    if prev and s == 11:
                        a = at.shift(-1)
                        sc.wait_ge(ftp_done, a.t + 1)
                        sc.activation(xfT[:, 0, :], pSTG[:, 0:TOK], ACT.Copy).then_inc(xfT_done, 1)
                        sc.activation(xfT[0:64, 1, :], pSTG[0:64, TOK:2 * TOK], ACT.Copy).then_inc(xfT_done, 1)
                    if prev and s == 10:
                        a = at.shift(-1)
                        sc.wait_ge(z32_done, 2 * (a.t + 1))
                        if not (isinstance(a.half, int) and a.half == 0):
                            sc.wait_ge(scattered[a.par], 64 * a.half)
                        sc.activation(zrow[:, a.par, :, 0:E // 2].bitcast(F16), z32[:], ACT.Copy).then_inc(zh_done, 1)

            over_steps(sc, step)

            def silu(q, k):
                sc.wait_ge(gu_done, q + 1)
                if not (isinstance(q, int) and q < 2):
                    wait(sc, mul_done, q - 1)
                sc.activation(sg[:, k % 2, :], banks[:, 2 * (k % 2), 0:CHUNK], ACT.Silu, scale=1.0 / W13S).then_inc(silu_done, 1)

            def high_a(q, pc, k):
                sc.wait_ge(mul_done, q + 1)
                sc.activation(act[:, pc, 0, k, :], a32[:, k % 2, :], ACT.Copy).then_inc(a_hi, 1)

            def z_parts(c, pc):
                sc.wait_ge(ft_done, c + 1)
                sc.activation(zT[:, pc, 0:2, :], zbank[:, 0:1024].rearrange("p (a s) -> p a s", a=2)[:, :, 0:CHUNK],
                              ACT.Copy).then_inc(zt_a, 1)

            z_parts(0, 0)
            silu(0, 0)
            high_a(0, 0, 0)

            def chunk(c, pc, i, e, pe_, nxt, unit):
                silu(4 * c + 1, 1)
                high_a(4 * c + 1, pc, 1)
                if nxt is not None:
                    z_parts(c + 1, 1 - pc)
                silu(4 * c + 2, 0)
                if unit:
                    unit13(c + PER_EXPERT, 1 - pe_, 2 * i + pc, e + 1)
                high_a(4 * c + 2, pc, 2)
                silu(4 * c + 3, 1)
                if unit:
                    unit2(c + PER_EXPERT, pc, 1 - pe_, i)
                high_a(4 * c + 3, pc, 3)
                if nxt is not None:
                    silu(4 * c + 4, 0)
                    high_a(4 * c + 4, 1 - pc, 0)
                if not (isinstance(c, int) and c < 2):
                    wait(sc, y_out[pc], 40 * c - 40 * pc)
                sc.wait_ge(meta_ready, 2 * (c + 1))
                for u, tiles in enumerate(((0, 1), (2, 3), (4,))):
                    sc.wait_ge(y_done, 3 * c + u + 1)
                    for n, m in enumerate(tiles):
                        ev = sc.activation(yout[:, pc, m, :], banks[0:R, 6 + (pc + u) % 2, E * n:E * n + E], ACT.Copy,
                                           scale=cw[:, pc, m:m + 1])
                    ev.then_inc(y_ev, 1)

            over_chunks(sc, chunk)

        @block.vector
        def _(ve):
            ve.wait_ge(pt_done, 1)
            ve.tensor_copy(q2[:], pT[:, 32:56].rearrange("p (a b) -> p a b", a=2)).then_inc(route, 1)
            ve.wait_ge(route, 1)
            ve.scalar_tensor_tensor(out=q2[:], in0=q2[:], scalar=QS, in1=q2[:], op0=ALU.mult, op1=ALU.mult).then_inc(pt_dve, 1)
            wte_next = [0]

            def wte_rows():
                k = wte_next[0]
                if k < WCHUNKS:
                    ve.wait_ge(w_in[k % 3], 16 * (k // 3 + 1))
                    if k >= 2:
                        ve.wait_ge(w_sum, k - 1)
                    ve.tensor_reduce(wpart[:, k % 2, :], stream[:, k % 3, :].rearrange("p (r e) -> p e r", e=E), AX.X, ALU.add).then_inc(w_red, 1)
                    wte_next[0] += 1

            wte_rows()
            wte_rows()
            for n in range(3 * PAIRS):
                ve.wait_ge(pt_act, 11 + n)
                ve.scalar_tensor_tensor(out=wo[:, 1, n, :], in0=banks[:, n % 2, 0:E], scalar=WOS, in1=wo[:, 0, n, :],
                                        op0=ALU.mult, op1=ALU.subtract).then_inc(pt_dve, 1)
                if n % 3 == 2:
                    wte_rows()
            def unit13(v, pe_, blk, e):
                ve.wait_ge(u13_hi, 2 * v + 2)
                for ab in (0, 1):
                    ve.scalar_tensor_tensor(out=w13t[:, pe_, 2 * ab + 1, bass.ds(blk * 128, 128)], in0=prep[:, 128 * ab:128 * ab + 128],
                                            scalar=nwT[:, ab, bass.ds(e, 1)], in1=w13t[:, pe_, 2 * ab, bass.ds(blk * 128, 128)],
                                            op0=ALU.mult, op1=ALU.subtract).then_inc(u13_lo, 1)

            def unit2(v, pc, pe_, i):
                ve.wait_ge(u2_hi, v + 1)
                hi, lo = (w2t[:, pe_, n, bass.ds(i, 1), 96 * pc:96 * pc + 96].rearrange("p o d -> p (o d)") for n in (0, 1))
                ve.scalar_tensor_tensor(out=lo, in0=prep[:, 0:96], scalar=W2S, in1=hi,
                                        op0=ALU.mult, op1=ALU.subtract).then_inc(u2_lo, 1)

            for v in range(PER_EXPERT):
                unit13(v, 0, v, 0)
                unit2(v, v % 2, 0, v // 2)
                for _ in range(2):
                    wte_rows()
            while wte_next[0] < WCHUNKS:
                wte_rows()

            def softmax_max(at, h):
                ve.wait_ge(s_done, heads(at, h))
                for half in (0, 1):
                    ve.tensor_reduce(mx[:, h % 2, half:half + 1], banks[0:R, h % 2, R * half:R * half + R * (half + 1)],
                                     AX.X, ALU.max).then_inc(max_done, 1)

            def low_l(at, h):
                n = 2 * heads(at, h)
                ve.wait_ge(lhi, n - 1)
                if h == 0:
                    ve.wait_ge(xt32_done, at.t + 1)
                Lh = L[:, h % 3]
                ve.scalar_tensor_tensor(out=Lh[:, 1, :], in0=xT[:, at.par, 0, :], scalar=q2[:, 0, h:h + 1], in1=Lh[:, 0, :],
                                        op0=ALU.mult, op1=ALU.subtract)
                ve.wait_ge(lhi, n)
                ve.scalar_tensor_tensor(out=Lh[64:128, 2, :], in0=xT[64:128, at.par, 1, :], scalar=q2[64:128, 1, h:h + 1],
                                        in1=Lh[64:128, 2, :], op0=ALU.mult, op1=ALU.subtract).then_inc(l_ready, 1)

            def turned(at, k, there):
                if there:
                    a, h = head_at(at, k)
                    ve.wait_ge(pt_hi, heads(a, h))
                    ve.tensor_tensor(PT[:, (h // 2) % 2, 1, h % 2, :], pT[0:R, 0:3 * R], PT[:, (h // 2) % 2, 0, h % 2, :],
                                     ALU.subtract).then_inc(pt_lo, 1)

            def lg(half):
                return pSTG[0:R, LG + 8 * half:LG + 8 * half + 8]

            def step(at, nxt, main, prev, prev2):
                up, down, past = at.shift(1), at.shift(-1), at.shift(-2)
                rt = 15 * past.t + 1
                for s in range(HEADS):
                    a, h = head_at(at, s - 1)
                    soft = (main if s >= 1 else prev)
                    if soft:
                        softmax_max(a, h)
                    a2, h_ = head_at(at, s - 2)
                    if (main if s >= 2 else prev):
                        ve.wait_ge(exp_done, 2 * heads(a2, h_))
                        ve.reciprocal(rinv[:, h_ % 4, :], sums[:, h_ % 4, :]).then_inc(r_ready, 1)
                    if soft:
                        ve.wait_ge(max_done, 2 * heads(a, h))
                        ve.tensor_scalar(nm[:, h % 2, :], mx[:, h % 2, :], -SC, None, ALU.mult).then_inc(nm_ready, 1)
                    if (main if s < HEADS - 1 else nxt):
                        low_l(*head_at(at, s + 1))
                    turned(at, s - 4, main if s >= 4 else prev)
                    if prev and s == 6:
                        ve.wait_ge(hcopy_done, down.t + 1)
                        ve.wait_ge(pj_done, down.t + 1)
                        ve.scalar_tensor_tensor(out=h2[:, down.par].rearrange("p a e -> p (a e)"), in0=pPJ[0:R, 0:2 * E],
                                                scalar=ATT, in1=h2[:, down.par].rearrange("p a e -> p (a e)"),
                                                op0=ALU.mult, op1=ALU.add).then_inc(h2_done, 1)
                    if prev and s == 6:
                        ve.wait_ge(h2_done, down.t + 1)
                        for half in (0, 1):
                            ve.bn_stats(st3[:, half, :], h2[:, down.par, half, :]).then_inc(bn3, 1)
                    if prev and s == 7:
                        wait_first(ve, bn3, 2 * (down.t + 1))
                        for half in (0, 1):
                            ve.bn_aggr(mv3[:, half, :], st3[:, half, :]).then_inc(stat3, 1)
                    if prev and s == 8:
                        ve.wait_ge(r3_done, down.t + 1)
                        for half in (0, 1):
                            ve.tensor_scalar(xf[:, down.par, half, :], h2[:, down.par, half, :], mv3[:, half, 0:1],
                                             pw3[:, 1, half:half + 1], ALU.subtract, ALU.mult).then_inc(xf_done, 1)
                    if prev and s == 9:
                        ve.wait_ge(xf_done, 2 * (down.t + 1))
                        ve.wait_ge(zs_done, down.t + 1)
                        wait(ve, zl_done, 2 * down.t)
                        for half in (0, 1):
                            ve.tensor_scalar(z32[:, half, :], xf[:, down.par, half, :], pw3[:, 6, half:half + 1],
                                             None, ALU.mult).then_inc(z32_done, 1)
                    if prev and s == 11:
                        ve.wait_ge(zh_done, down.t + 1)
                        zr = zrow[:, down.par, :, 0:E].bitcast(F16)
                        ve.tensor_tensor(zr[:, :, 256:384], z32[:, :, 0:128], zr[:, :, 0:128], ALU.subtract).then_inc(zl_done, 1)
                        ve.tensor_tensor(zr[:, :, E:256], z32[:, :, 128:E], zr[:, :, 128:E], ALU.subtract).then_inc(zl_done, 1)
                    if nxt and s == 4:
                        ve.wait_ge(tok_done, up.t + 1)
                        wait(ve, hcopy_done, up.t - 1)
                        if isinstance(up.t, int) and up.t == 0:
                            ve.wait_ge(bc_in, 32)
                        ve.tensor_tensor(hbuf[:, up.par], pACC[0:R, 0:2 * E].rearrange("p (a e) -> p a e", a=2),
                                         btok[:].rearrange("p (o e) -> p o e", o=1).to_broadcast([R, 2, E]), ALU.add).then_inc(h_done, 1)
                    if nxt and s == 5:
                        ve.wait_ge(h_done, up.t + 1)
                        for half in (0, 1):
                            ve.bn_stats(st1[:, half, :], hbuf[:, up.par, half, :]).then_inc(pre_dve, 1)
                        wait_first(ve, pre_dve, 2 * (up.t + 1))
                        for half in (0, 1):
                            ve.bn_aggr(mv1[:, half, :], st1[:, half, :]).then_inc(stat1, 1)
                    if nxt and s == 7:
                        ve.wait_ge(r1_done, up.t + 1)
                        wait(ve, xn_done, 3 * up.t)
                        wait(ve, v32_done, up.t)
                        wait(ve, xtp_done, up.t)
                        for half in (0, 1):
                            ve.tensor_scalar(xn[:, half, 0:E], hbuf[:, up.par, half, :], mv1[:, half, 0:1],
                                             pw1[:, 5, half:half + 1], ALU.subtract, ALU.mult).then_inc(xn_done, 1)
                        ve.wait_ge(xn_done, 3 * up.t + 2)
                        ve.tensor_tensor(xn[:, :, 0:E], xn[:, :, 0:E], lnw[:].rearrange("p (o e) -> p o e", o=1).to_broadcast([R, 2, E]),
                                         ALU.mult).then_inc(xn_done, 1)
                    if nxt and s == 10:
                        ve.wait_ge(xth_done, up.t + 1)
                        ve.tensor_tensor(XT[:, up.par, 1], pSTG[:, 0:2 * TOK].rearrange("p (a s) -> p a s", a=2), XT[:, up.par, 0],
                                         ALU.subtract).then_inc(xtl_done, 1)
                    if nxt and s == 11:
                        ve.wait_ge(vh_done, up.t + 1)
                        ve.tensor_tensor(V[:, up.par, 1, :, 0:E], V32[:], V[:, up.par, 0, :, 0:E], ALU.subtract).then_inc(vl_done, 1)
                    if prev2:
                        if s == 1:
                            wait_first(ve, lg_done, past.t + 1)
                            for half in (0, 1):
                                ve.max(top[:, half, :], lg(half)).then_inc(route, 1)
                        if s == 1:
                            wait_first(ve, route, rt + 2)
                            for half in (0, 1):
                                ve.max_index(topi[:, half, :], top[:, half, :], lg(half)).then_inc(route, 1)
                            ve.tensor_tensor(dif[:], top[:, :, 1], top[:, :, 0], ALU.subtract).then_inc(route, 1)
                        if s == 2:
                            ve.wait_ge(route, rt + 5)
                            ve.tensor_copy(topf[:], topi[:, :, 0:2]).then_inc(route, 1)
                        if s == 3:
                            ve.wait_ge(route, rt + 6)
                            for half in (0, 1):
                                ve.tensor_tensor(oh[:, half], iota8[:].rearrange("p (o e) -> p o e", o=1).to_broadcast([R, 2, EXPERTS]),
                                                 topf[:, half].rearrange("p (k o) -> p k o", o=1).to_broadcast([R, 2, EXPERTS]),
                                                 ALU.is_equal).then_inc(route, 1)
                            ve.wait_ge(e_done, past.t + 1)
                            ve.tensor_scalar(eden[:], edif[:], 1.0, None, ALU.add).then_inc(route, 1)
                        if s == 4:
                            ve.wait_ge(route, rt + 9)
                            wait(ve, meta_done, 2 * past.t)
                            ve.tensor_tensor(both[:], oh[:, :, 0, :], oh[:, :, 1, :], ALU.add).then_inc(both_done, 1)
                            ve.reciprocal(wk[:, :, 0], eden[:]).then_inc(route, 1)
                        if s == 5:
                            ve.wait_ge(route, rt + 10)
                            ve.tensor_tensor(wk[:, :, 1], edif[:], wk[:, :, 0], ALU.mult).then_inc(route, 1)
                        if s == 6:
                            ve.wait_ge(cu_done, past.t + 1)
                            ve.tensor_tensor(place[:], pSTG[0:R, CU:CU + 16].rearrange("p (a b) -> p a b", a=2),
                                             base[:].rearrange("p (o e) -> p o e", o=1).to_broadcast([R, 2, EXPERTS]), ALU.add).then_inc(route, 1)
                            ve.wait_ge(route, rt + 12)
                            ve.tensor_tensor(base[:], pSTG[0:R, CU + 16:CU + 24], base[:], ALU.add).then_inc(route, 1)
                            ve.tensor_tensor(over[:], place[:], limit[:].rearrange("p (o e) -> p o e", o=1).to_broadcast([R, 2, EXPERTS]),
                                             ALU.is_ge).then_inc(route, 1)
                        if s == 7:
                            ve.wait_ge(route, rt + 14)
                            ve.scalar_tensor_tensor(out=place[:], in0=over[:], scalar=BIG, in1=place[:], op0=ALU.mult, op1=ALU.add
                                                    ).then_inc(route, 1)
                            ve.wait_ge(route, rt + 15)
                            wait(ve, slot_done, 7 * past.t)
                            for k in (0, 1):
                                ve.tensor_tensor(picked[:, :, k, :], oh[:, :, k, :], place[:], ALU.mult).then_inc(slot_done, 1)
                        if s == 9:
                            ve.wait_ge(slot_done, 7 * past.t + 2)
                            ve.tensor_reduce(slot[:], picked[:], AX.X, ALU.add).then_inc(slot_done, 1)
                            ve.wait_ge(slot_done, 7 * past.t + 3)
                            if not (isinstance(past.half, int) and past.half == 0):
                                ve.wait_ge(scattered[past.par], 64 * past.half)
                            ve.tensor_copy(sloti[:, past.par], slot[:]).then_inc(slot_done, 1)
                            for half in (0, 1):
                                ve.scalar_tensor_tensor(out=kept[:, half, :], in0=slot[:, half, :], scalar=BIG, in1=wk[:, half, :],
                                                        op0=ALU.is_lt, op1=ALU.mult).then_inc(slot_done, 1)
                        if s == 10:
                            ve.wait_ge(slot_done, 7 * past.t + 6)
                            ve.tensor_tensor(kw[:], kept[:, :, 0], kept[:, :, 1], ALU.add).then_inc(slot_done, 1)
                        if s == 11:
                            ve.wait_ge(slot_done, 7 * past.t + 7)
                            if not (isinstance(past.half, int) and past.half == 0):
                                ve.wait_ge(hout_out[past.par], 16 * past.half)
                            for half in (0, 1):
                                ve.scalar_tensor_tensor(out=hout[:, past.par, half, :], in0=xf[:, past.par, half, :], scalar=kw[:, half:half + 1],
                                                        in1=h2[:, past.par, half, :], op0=ALU.mult, op1=ALU.add).then_inc(hout_done, 1)
                    q = (s - 6) // 2
                    if s % 2 == 0 and (main if q >= 0 else prev):
                        a, k = at.shift(q // PAIRS), q % PAIRS
                        ve.wait_ge(ot_hi, 2 * pairs(a, k))
                        ve.scalar_tensor_tensor(out=OT[:, k % 2, 1, 0:2, :].rearrange("p h s -> p (h s)"), in0=pOA[:, 0:2 * TOK], scalar=OS,
                                                in1=OT[:, k % 2, 0, 0:2, :].rearrange("p h s -> p (h s)"),
                                                op0=ALU.mult, op1=ALU.subtract).then_inc(ot_lo, 1)
                        ve.scalar_tensor_tensor(out=OT[:, k % 2, 1, 2, :], in0=pOB[:, 0:TOK], scalar=OS, in1=OT[:, k % 2, 0, 2, :],
                                                op0=ALU.mult, op1=ALU.subtract).then_inc(ot_lo, 1)

            over_steps(ve, step)

            def z_rest(c, pc):
                ve.wait_ge(ft_done, c + 1)
                ve.tensor_copy(zT[:, pc, 2, :], zbank[:, 1024:1024 + CHUNK]).then_inc(zt_b, 1)
                wait(ve, first_done, 2 * c)
                ve.tensor_tensor(isfirst[:, pc, :], rows[:, pc, :, META_SLOT], slotid[:], ALU.is_equal).then_inc(first_done, 1)
                ve.wait_ge(first_done, 2 * c + 1)
                ve.tensor_scalar(slotid[:], slotid[:], float(CHUNK), None, ALU.add).then_inc(first_done, 1)

            def gate(q, k):
                ve.wait_ge(silu_done, q + 1)
                if not (isinstance(q, int) and q < 2):
                    wait(ve, a_lo, q - 1)
                ve.tensor_tensor(a32[:, k % 2, :], banks[:, 2 * (k % 2) + 1, 0:CHUNK], sg[:, k % 2, :], ALU.mult).then_inc(mul_done, 1)

            def low_a(q, pc, k):
                ve.wait_ge(a_hi, q + 1)
                ve.tensor_tensor(act[:, pc, 1, k, :], a32[:, k % 2, :], act[:, pc, 0, k, :], ALU.subtract).then_inc(a_lo, 1)

            z_rest(0, 0)
            gate(0, 0)
            low_a(0, 0, 0)

            def chunk(c, pc, i, e, pe_, nxt, unit):
                gate(4 * c + 1, 1)
                if nxt is not None:
                    z_rest(c + 1, 1 - pc)
                low_a(4 * c + 1, pc, 1)
                gate(4 * c + 2, 0)
                if unit:
                    unit13(c + PER_EXPERT, 1 - pe_, 2 * i + pc, e + 1)
                low_a(4 * c + 2, pc, 2)
                gate(4 * c + 3, 1)
                if unit:
                    unit2(c + PER_EXPERT, pc, 1 - pe_, i)
                low_a(4 * c + 3, pc, 3)
                if nxt is not None:
                    gate(4 * c + 4, 0)
                    low_a(4 * c + 4, 1 - pc, 0)

            over_chunks(ve, chunk)

        @block.gpsimd
        def _(po):
            class Order:

                def __init__(self, s, start=0):
                    self.s, self.n = s, start

                def __call__(self, ins):
                    self.n = self.n + 1
                    ins.then_inc(self.s, 1)
                    wait_first(po, self.s, self.n)

            own = Order(pool_order)

            def select(t, op, fill, b, cm, step_, width):
                return po.affine_select(out=t, in_=t, compare_op=op, fill=fill, base=b, pattern=[[step_, width]], channel_multiplier=cm)

            own(po.memset(empty[:], 0.0))
            own(po.iota(iotai[:, 10:15], pattern=[[1, 5]], base=0, channel_multiplier=5))
            own(po.tensor_copy(slotid[:], iotai[:, 10:15]))
            po.tensor_scalar(empty[:, :, META_N], slotid[:], float(N), None, ALU.add).then_inc(fill_ready, 1)
            own(po.memset(halfneg[:], -0.5))
            own(po.memset(ones32[:], 1.0))
            own(po.memset(ones16[:], 1.0))
            own(po.memset(id32[:], 0.0))
            own(select(id32[:], ALU.not_equal, 1.0, 0, 1, -1, 128))
            own(po.memset(id16[:], 0.0))
            own(select(id16[:], ALU.not_equal, 1.0, 0, 1, -1, 128))
            own(po.memset(idbf[:], 0.0))
            own(select(idbf[:], ALU.not_equal, 1.0, 0, 1, -1, R))
            own(po.memset(maskbf[:], 0.0))
            own(select(maskbf[:], ALU.is_ge, -1e30, 0, 1, -1, R))
            own(po.memset(before[:], 0.0))
            own(select(before[:], ALU.is_ge, 1.0, 0, 1, -1, R))
            own(po.memset(V[:], 0.0))
            own(po.iota(iotai[:, 0:8], pattern=[[1, 8]], base=0, channel_multiplier=0))
            own(po.tensor_copy(iota8[:], iotai[:, 0:8]))
            own(po.iota(iotai[:, 0:8], pattern=[[CAP, 8]], base=0, channel_multiplier=0))
            own(po.tensor_copy(base[:], iotai[:, 0:8]))
            own(po.tensor_scalar(limit[:], base[:], float(CAP), None, ALU.add))
            own(po.iota(iotai[:, 8:10], pattern=[[R, 2]], base=0, channel_multiplier=1))
            own(po.tensor_copy(tokid[:], iotai[:, 8:10]))
            own(po.tensor_scalar(nreg[:], tokid[:], 1.0, None, ALU.add))
            own(po.memset(pw1[:, 0, :], -1.0))
            own(po.tensor_tensor(nreg[:], nreg[:], pw1[:, 0, :], ALU.pow))
            po.tensor_scalar(nreg[:], nreg[:], PS, None, ALU.mult).then_inc(c_ready, 1)
            po.wait_ge(c_ready, 1)
            po.wait_ge(pt_dve, 1)
            po.wait_ge(pt_act, 2 + 8 + 3 * PAIRS + 1)

            def step(at, nxt, main, prev, prev2):
                up, down, past = at.shift(1), at.shift(-1), at.shift(-2)
                for s in range(HEADS):
                    a, h = head_at(at, s - 2)
                    if (main if s >= 2 else prev):
                        wait_first(po, r_ready, heads(a, h))
                        for half in (0, 1):
                            cols = slice(R * half, R * half + R * (half + 1))
                            po.tensor_scalar(P[:, h % 4, cols], P[:, h % 4, cols], rinv[:, h % 4, half:half + 1],
                                             nreg[:, half:half + 1], ALU.mult, ALU.mult).then_inc(n_done, 1)
                    if prev and s == 7:
                        wait_first(po, stat3, 2 * (down.t + 1))
                        v = mv3[:, :, 1]
                        own = Order(post_pool, 5 * down.t)
                        own(po.tensor_scalar(pw3[:, 0, :], v, 1e-5, None, ALU.add))
                        po.tensor_tensor(pw3[:, 1, :], pw3[:, 0, :], halfneg[:, 0:2], ALU.pow).then_inc(r3_done, 1)
                        wait_first(po, r3_done, down.t + 1)
                        own(po.tensor_tensor(pw3[:, 2, :], pw3[:, 1, :], pw3[:, 1, :], ALU.mult))
                        own(po.tensor_tensor(pw3[:, 3, :], pw3[:, 2, :], v, ALU.mult))
                        own(po.tensor_scalar(pw3[:, 4, :], pw3[:, 3, :], 4.0, 1e-6, ALU.mult, ALU.add))
                        own(po.tensor_tensor(pw3[:, 5, :], pw3[:, 4, :], halfneg[:, 0:2], ALU.pow))
                        po.tensor_scalar(pw3[:, 6, :], pw3[:, 5, :], 2.0, None, ALU.mult).then_inc(zs_done, 1)
                    if nxt and s == 6:
                        wait_first(po, stat1, 2 * (up.t + 1))
                        v = mv1[:, :, 1]
                        own = Order(pre_pool, 6 * up.t)
                        own(po.tensor_scalar(pw1[:, 0, :], v, 1e-5, None, ALU.add))
                        own(po.tensor_tensor(pw1[:, 1, :], pw1[:, 0, :], halfneg[:, 0:2], ALU.pow))
                        own(po.tensor_tensor(pw1[:, 2, :], pw1[:, 1, :], pw1[:, 1, :], ALU.mult))
                        own(po.tensor_tensor(pw1[:, 3, :], pw1[:, 2, :], v, ALU.mult))
                        own(po.tensor_scalar(pw1[:, 2, :], pw1[:, 3, :], 1e-5, None, ALU.add))
                        own(po.tensor_tensor(pw1[:, 4, :], pw1[:, 2, :], halfneg[:, 0:2], ALU.pow))
                        po.tensor_tensor(pw1[:, 5, :], pw1[:, 4, :], pw1[:, 1, :], ALU.mult).then_inc(r1_done, 1)
                    if nxt and s == 8:
                        wait_first(po, xn_done, 3 * (up.t + 1))
                        po.tensor_copy(xn[:, :, E:256], xn[:, :, 128:E]).then_inc(dup_done, 1)
                        wait_first(po, vl_done, up.t)
                        po.tensor_tensor(V32[:], xn[:, :, 0:E], avg[:].rearrange("p (o e) -> p o e", o=1).to_broadcast([R, 2, E]),
                                         ALU.subtract).then_inc(v32_done, 1)
                    if nxt and s == 9:
                        wait_first(po, v32_done, up.t + 1)
                        wait_first(po, ot_done, PAIRS * (up.t - 1))
                        po.tensor_copy(V[:, up.par, 0, :, 0:E], V32[:]).then_inc(vh_done, 1)
                        po.tensor_copy(V[:, up.par, 0, :, 256:320], V32[:, :, 128:E]).then_inc(v_ready, 1)
                    if main and s == 0:
                        wait_first(po, vl_done, at.t + 1)
                        po.tensor_copy(V[:, at.par, 1, :, 256:320], V[:, at.par, 1, :, 128:E]).then_inc(v_ready, 1)
                    if prev and s == 0:
                        wait_first(po, h_done, down.t + 1)
                        if not (isinstance(down.t, int) and down.t < 2):
                            wait_first(po, hout_done, 2 * (down.t - 1))
                        po.tensor_copy(h2[:, down.par], hbuf[:, down.par]).then_inc(hcopy_done, 1)
                    if isinstance(at.t, int) and at.t == 1 and s == 11:
                        wait_first(po, empty_out, 16 * CHUNKS)
                    if prev2 and s == 10:
                        wait_first(po, slot_done, 7 * past.t + 4)
                        po.tensor_copy(zrow[:, past.par, :, META_N], tokid[:])
                        po.tensor_copy(zrow[:, past.par, :, META_SLOT], slot[:, :, 0])
                        po.tensor_copy(zrow[:, past.par, :, META_W:META_W + 2], wk[:]).then_inc(meta_done, 1)
                        wait_first(po, meta_done, 2 * past.t + 1)
                        po.tensor_scalar(tokid[:], tokid[:], float(TOK), None, ALU.add).then_inc(meta_done, 1)
                        wait_first(po, zl_done, 2 * (past.t + 1))
                        for half in (0, 1):
                            for k in (0, 1):
                                po.indirect_dma_start(BUF, bass.IndirectOffsetOnAxis(ap=sloti[:, past.par, half, k:k + 1], axis=0),
                                                      zrow[:, past.par, half, :], None, bounds_check=SLOTS - 1,
                                                      oob_is_err=False).then_inc(scattered[past.par], 16)

            over_steps(po, step)

            def meta(c, pc):
                wait_first(po, first_done, 2 * c + 1)
                own = Order(meta_step, 4 * c)
                own(po.tensor_scalar(eq[:, 1, :], isfirst[:, pc, :], -1.0, 1.0, ALU.mult, ALU.add))
                own(po.tensor_tensor(eq[:, 2, :], isfirst[:, pc, :], rows[:, pc, :, META_W], ALU.mult))
                own(po.tensor_tensor(eq[:, 0, :], eq[:, 1, :], rows[:, pc, :, META_W + 1], ALU.mult))
                own(po.tensor_tensor(eq[:, 2, :], eq[:, 2, :], eq[:, 0, :], ALU.add))
                if not (isinstance(c, int) and c < 2):
                    wait_first(po, y_out[pc], 40 * c - 40 * pc)
                po.tensor_copy(desti[:, pc, :, 0], rows[:, pc, :, META_N]).then_inc(meta_ready, 1)
                po.tensor_scalar(cw[:, pc, :], eq[:, 2, :], 1.0 / (W13S * W2S), None, ALU.mult).then_inc(meta_ready, 1)

            meta(0, 0)

            def chunk(c, pc, i, e, pe_, nxt, unit):
                wait_first(po, y_ev, 3 * c + 3)
                wait_first(po, meta_ready, 2 * (c + 1))
                wait_first(po, y_out[1 - pc], 40 * (c + pc))
                for m in range(5):
                    po.indirect_dma_start(SUM, bass.IndirectOffsetOnAxis(ap=desti[:, pc, m, :], axis=0), yout[:, pc, m, :], None,
                                          bounds_check=N + CHUNK - 1, oob_is_err=True, compute_op=ALU.add).then_inc(y_out[pc], 16)
                if nxt is not None:
                    meta(c + 1, 1 - pc)

            for p in (0, 1):
                po.wait_ge(hout_out[p], 16 * (IMAGES // 2))
            over_chunks(po, chunk)


_INS = ["x", "L0_tok_W", "L0_tok_b", "L0_attn_ln_w", "L0_attn_W_qk", "L0_attn_W_o", "L0_attn_wte",
        "L0_ffn_gate_w", "L0_ffn_w13", "L0_ffn_w2", "L0_ffn_norm_w"]


def kernel(**inputs):
    import numpy as np
    import concourse.bacc as bacc
    from concourse import mybir as mb
    from concourse.bass_utils import run_bass_kernel_spmd

    nc = bacc.Bacc("TRN2", target_bir_lowering=False, num_devices=1)
    arrays, args = {}, []
    for name in _INS:
        a = np.ascontiguousarray(inputs[name])
        arrays[name] = a
        args.append(nc.dram_tensor(name, a.shape, mb.dt.from_np(a.dtype), kind="ExternalInput").ap())
    args.append(nc.dram_tensor("out", (IMAGES, TOK, E), mb.dt.float32, kind="ExternalOutput").ap())
    build(nc, *args)
    r = run_bass_kernel_spmd(nc, [arrays], core_ids=[0])
    return r.results[0]["out"]
```
